# Optimizing a Trainium2 kernel written in Bass

```python
import numpy as np
import jax
import jax.numpy as jnp

def _softmax(x, axis=-1):
    return jax.nn.softmax(x, axis=axis)

def _gelu(x):
    return jax.nn.gelu(x, approximate=True)

def _silu(x):
    return jax.nn.silu(x)

def _sigmoid(x):
    return jax.nn.sigmoid(x)

def _layernorm(x, axis=-1, eps=1e-05):
    m = jnp.mean(x, axis=axis, keepdims=True)
    v = jnp.var(x, axis=axis, keepdims=True)
    return (x - m) / jnp.sqrt(v + eps)

def _scatter_add(tgt, idx, src, axis=0):
    return tgt.at[idx].add(src)

def _segment_sum(src, seg, n):
    return jax.ops.segment_sum(src, seg, n)
kernel_name = 'mk_gnn_resnorm_d2_gnn_r32_2dc7b6'

def setup_inputs(seed: int=0):
    np.random.seed(seed)
    _w = jnp.asarray

    def _rec_inputs():
        import jax
        import jax.numpy as jnp
        _gk = jax.random.key(seed)
        x = -6.415e-05 + 1 * jax.random.normal(jax.random.fold_in(_gk, 1), (10000, 512), jnp.float32)
        src = jax.random.randint(jax.random.fold_in(_gk, 2), (5000,), 0, 10000, jnp.int32)
        dst = jax.random.randint(jax.random.fold_in(_gk, 3), (5000,), 0, 10000, jnp.int32)
        _o = jnp.argsort(dst, stable=True)
        src = src[_o]
        dst = dst[_o]
        edge_attr_512 = -8.16379e-05 + 0.999858 * jax.random.normal(jax.random.fold_in(_gk, 12), (5000, 512), jnp.float32)
        return (x, src, dst, edge_attr_512)
    x, src, dst, edge_attr_512 = _rec_inputs()

    def _L0_gnn_setup():
        import jax, jax.numpy as jnp
        import numpy as np
        N_NODES = 625
        N_EDGES = 6250
        N_SEG = 16
        EXTENT = 32
        N_PATHS = 64
        OP_SIZE = N_SEG * EXTENT
        key = jax.random.key(seed)
        k1, k2, k3, k4, k5, k6 = jax.random.split(key, 6)
        x_nodes = jax.random.normal(k1, (N_NODES, OP_SIZE), dtype=jnp.float32)
        x_edges = jax.random.normal(k2, (N_EDGES, OP_SIZE), dtype=jnp.float32)
        path_coeffs = jax.random.normal(k3, (N_PATHS,), dtype=jnp.float32)
        src = jax.random.randint(k4, (N_EDGES,), 0, N_NODES, dtype=jnp.int64)
        dst = jax.random.randint(k5, (N_EDGES,), 0, N_NODES, dtype=jnp.int64)
        path_indices = jax.random.randint(k6, (N_PATHS, 3), 0, N_SEG, dtype=jnp.int64)
        return {'x_nodes': x_nodes, 'x_edges': x_edges, 'path_coeffs': path_coeffs, 'src': src, 'dst': dst, 'path_indices': path_indices}
    _L0_gnn_all = _L0_gnn_setup()
    _L0_gnn_in = {k: v for k, v in _L0_gnn_all.items() if k in ('path_coeffs', 'path_indices')}
    del _L0_gnn_all

    def _L1_gnn_setup():
        import jax, jax.numpy as jnp
        import numpy as np
        N_NODES = 625
        N_EDGES = 150000
        D_IN = 512
        D_OUT = 512
        BN_EPS = 1e-05
        key = jax.random.key(seed)
        k1, k2, k3, k4 = jax.random.split(key, 4)
        x = jax.random.normal(k1, (N_NODES, D_IN), dtype=jnp.float32)
        src = jax.random.randint(k2, (N_EDGES,), 0, N_NODES, dtype=jnp.int64)
        dst = jax.random.randint(k3, (N_EDGES,), 0, N_NODES, dtype=jnp.int64)
        W = jax.random.normal(k4, (D_OUT, D_IN), dtype=jnp.float32) * (1.0 / np.sqrt(D_IN))
        b = jnp.zeros((D_OUT,), dtype=jnp.float32)
        gamma = jnp.ones((D_OUT,), dtype=jnp.float32)
        beta = jnp.zeros((D_OUT,), dtype=jnp.float32)
        return {'x': x, 'src': src, 'dst': dst, 'W': W, 'b': b, 'gamma': gamma, 'beta': beta}
    _L1_gnn_all = _L1_gnn_setup()
    _L1_gnn_in = {k: v for k, v in _L1_gnn_all.items() if k in ('W', 'b', 'gamma', 'beta')}
    del _L1_gnn_all
    return {'x': x, 'src': src, 'dst': dst, 'edge_attr_512': edge_attr_512, 'L0_gnn_path_coeffs': _L0_gnn_in['path_coeffs'], 'L0_gnn_path_indices': _L0_gnn_in['path_indices'], 'L1_gnn_W': _L1_gnn_in['W'], 'L1_gnn_b': _L1_gnn_in['b'], 'L1_gnn_gamma': _L1_gnn_in['gamma'], 'L1_gnn_beta': _L1_gnn_in['beta']}

def reference(x, src, dst, edge_attr_512, L0_gnn_path_coeffs, L0_gnn_path_indices, L1_gnn_W, L1_gnn_b, L1_gnn_gamma, L1_gnn_beta):
    import jax
    import jax.numpy as jnp

    def _L0_gnn_ref(x_nodes, x_edges, path_coeffs, src, dst, path_indices):
        import jax, jax.numpy as jnp
        import numpy as np
        N_NODES = 625
        N_EDGES = 6250
        N_SEG = 16
        EXTENT = 32
        N_PATHS = 64
        OP_SIZE = N_SEG * EXTENT
        n_nodes = x_nodes.shape[0]
        x1 = x_nodes[src].reshape(-1, N_SEG, EXTENT)
        x2 = x_edges.reshape(-1, N_SEG, EXTENT)
        i1, i2, i3 = (path_indices[:, 0], path_indices[:, 1], path_indices[:, 2])
        contrib = path_coeffs[None, :, None] * x1[:, i1, :] * x2[:, i2, :]
        edge_out = jnp.zeros((x2.shape[0], N_SEG, EXTENT), x_nodes.dtype).at[:, i3, :].add(contrib)
        out = jnp.zeros((n_nodes, OP_SIZE), x_nodes.dtype).at[dst].add(edge_out.reshape(-1, OP_SIZE))
        return out

    def _L1_gnn_ref(x, src, dst, W, b, gamma, beta):
        import jax, jax.numpy as jnp
        import numpy as np
        N_NODES = 625
        N_EDGES = 150000
        D_IN = 512
        D_OUT = 512
        BN_EPS = 1e-05
        n = x.shape[0]
        agg = jax.ops.segment_sum(x[src], dst, num_segments=n)
        indeg = jax.ops.segment_sum(jnp.ones(dst.shape, dtype=x.dtype), dst, num_segments=n)
        h = jnp.where(indeg[:, None] > 0, agg, x)
        h = jnp.einsum('nd,od->no', h, W) + b
        h = jax.nn.relu(h)
        mean = jnp.mean(h, axis=0)
        var = jnp.var(h, axis=0)
        h = (h - mean) * jax.lax.rsqrt(var + BN_EPS) * gamma + beta
        return h
    x = _layernorm(x + _L0_gnn_ref(x, edge_attr_512, L0_gnn_path_coeffs, src, dst, L0_gnn_path_indices), axis=-1)
    x = _layernorm(x + _L1_gnn_ref(x, src, dst, L1_gnn_W, L1_gnn_b, L1_gnn_gamma, L1_gnn_beta), axis=-1)
    return x

_drawn_inputs = setup_inputs


def setup_inputs(seed=0):
    import zlib

    import numpy as np

    out = dict(_drawn_inputs(seed))
    spreads = {'L1_gnn_b': (0.0, 0.1), 'L1_gnn_gamma': (1.0, 0.2), 'L1_gnn_beta': (0.0, 0.1)}
    factors = {}
    for name, (base, spread) in spreads.items():
        noise = np.random.default_rng([zlib.crc32(name.encode()), seed]).standard_normal(out[name].shape)
        drawn = base * np.exp(spread * noise) if base else spread * noise
        out[name] = jnp.asarray(drawn.astype(out[name].dtype))
    for name, factor in factors.items():
        out[name] = (out[name] * factor).astype(out[name].dtype)
    return out
```

```python
from contextlib import ExitStack

import concourse.bass as bass
from concourse import mybir

F32 = mybir.dt.float32
BF16 = mybir.dt.bfloat16
I32 = mybir.dt.int32
ALU = mybir.AluOpType
ACT = mybir.ActivationFunctionType
AX_X = mybir.AxisListType.X

P = 128
EPS = 1e-5
SEGS = 16


def build(nc, x, src, dst, edge_attr, coeffs, paths, W, b, gamma, beta, out):
    N, D = x.shape
    E = src.shape[0]
    NPATH = coeffs.shape[0]
    EXT = D // SEGS
    KD = D // P
    EPT = P - 1
    ET = 40
    assert (ET - 1) * EPT < E <= ET * EPT and E % ET == 0
    QL = P * (ET + 1)
    NT = -(-N // P)
    NFULL = N // P
    NREST = N - NFULL * P
    GT = 10
    NG = ET // GT
    GW = GT * D
    X = 6
    BIG = 1 << 20
    MISS = 1 << 20
    LAST_STEADY = (NFULL // X) - 1

    es = ExitStack()
    with es:
        def sb(name, shape, dt):
            return es.enter_context(nc.sbuf_tensor(name, shape, dt))

        def sem(name):
            return es.enter_context(nc.semaphore(name))

        def dram(name, shape, dt):
            return nc.dram_tensor(name, shape, dt, kind="Internal").ap()

        src_q = dram("src_q", (QL, 1), I32)
        dst_q = dram("dst_q", (QL, 1), I32)
        eid_q = dram("eid_q", (QL, 1), I32)
        sum0 = dram("sum0", (ET * P, D), F32)
        sum1 = dram("sum1", (ET * P, D), F32)
        x1_d = dram("x1_d", (N, D), F32)
        z_d = dram("z_d", (N, D), F32)

        def q_view(t, start, steps):
            return bass.AP(t.tensor, start, steps)

        arena = sb("arena", [P, NT * D], F32)
        zres = arena
        x_src = [arena[:, k * GW:(k + 1) * GW] for k in range(2)]
        x_edge = [arena[:, (2 + k) * GW:(3 + k) * GW] for k in range(2)]
        msg = [arena[:, (4 + k) * GW:(5 + k) * GW] for k in range(2)]
        msg_tiles = arena[:, 4 * GW:6 * GW]
        w_at = 6 * GW
        prod_at = w_at + KD * D
        prod = [arena[:, prod_at + k * GT * EXT:prod_at + (k + 1) * GT * EXT] for k in range(4)]
        coef_at = prod_at + 4 * GT * EXT
        coef = arena[:, coef_at:coef_at + NPATH]
        U = 4
        path_i = arena[0:1, coef_at + NPATH:coef_at + 4 * NPATH + 3 * U].bitcast(I32)
        assert coef_at + 4 * NPATH + 3 * U <= NT * D and NPATH % (2 * U) == 0
        QB = ET * P + 1
        dst_bi = arena[:, 0:QB].bitcast(I32)
        dst_b = arena[:, QB + 1:2 * QB + 1]
        place_b = arena[:, 2 * QB + 2:3 * QB + 1]
        less_b = arena[:, 3 * QB + 2:4 * QB + 1]
        scr_b = arena[:, 4 * QB + 2:5 * QB + 1]
        wload = arena[:, w_at:w_at + KD * D].rearrange("p (c i) -> p c i", c=KD)
        assert 5 * QB + 2 <= w_at

        same16 = sb("same16", [P, ET, P], BF16)
        same = sb("same", [P, 2, P], F32)
        WT = sb("WT", [P, KD, D], F32)
        negb = sb("negb", [P, D], F32)
        acc = sb("acc", [P, 2, D], F32)
        sq = sb("sq", [P, 2, D], F32)
        ring = sb("ring", [P, X, D], F32)
        xT = sb("xT", [P, 2, KD, P], F32)
        ident = sb("ident", [P, P], F32)
        ident0 = sb("ident0", [P, P], F32)
        cols = sb("cols", [P, 8, ET], F32)
        cols_i = sb("cols_i", [P, 3, ET], I32)
        noedge = sb("noedge", [P, NT], F32)
        node_row = sb("node_row", [P, NT], I32)
        stat6 = sb("stat6", [P, 6], F32)
        mv = sb("mv", [P, 2 * X], F32)
        stdv = sb("stdv", [P, X], F32)
        rstd = sb("rstd", [P, X], F32)
        nmr = sb("nmr", [P, X], F32)
        ones = sb("ones", [P, P], F32)
        epsc = sb("epsc", [P, 1], F32)
        bn_a, bn_c, bn_m, bn_t = (WT[:, k, :] for k in range(4))
        rows_i = sq[0:ET, 0, 0:3 * (P + 1)].bitcast(I32).rearrange("t (a p) -> t a p", a=3)
        rows_f = ring[0:ET, 0:3, 0:P + 1]
        derived = ring[0:ET, 3:5, :].rearrange("t a (c p) -> t (a c) p", p=P)
        der_i = xT[0:ET, 0, :, :].bitcast(I32)
        hot = xT[:, 1, :, :]
        tab_f = sq[:, 0, 0:NT]
        iota_f = acc[:, 0, 0:P]
        sort_i = acc[:, 1, 0:4 * ET].bitcast(I32).rearrange("p (a t) -> p a t", a=4)
        sort_f = sq[:, 1, 0:4 * ET].rearrange("p (a t) -> p a t", a=4)
        pad_i = xT[0:1, 0, 0, 0:128].bitcast(I32)
        zero_i = xT[0:1, 0, 1, 0:128].bitcast(I32)
        eid_i = ring[0:E // ET, 5, 0:ET].bitcast(I32)
        flag_f = sb("flag_f", [P, 2], F32)
        flag_i = sb("flag_i", [1, 1], I32)

        def bank(name):
            return es.enter_context(nc.psum_tensor(name, [P, D], F32))

        p_t = [bank("p_t0"), bank("p_t1")]
        p_z = [bank("p_z0"), bank("p_z1")]
        p_sum = [bank("p_sum0"), bank("p_sum1")]
        p_misc = bank("p_misc")
        p_tab = bank("p_tab")

        S = {n: sem(n) for n in (
            "consts", "small_loaded", "w_loaded", "pads_ready", "list_filled", "first_rows", "edge_rows", "dstb_loaded",
            "prep_v", "flag_sum", "flag_ready", "sort_loaded", "rank_ready", "scattered", "sort_v",
            "edges_final", "cols_ready", "hot_ready", "hot_used", "table_sum", "tables_ready", "wt_psum", "wt_ready",
            "same_ready", "sum_done", "carry_ready", "sum_out", "path_ready", "prod_done", "path_done", "group_zeroed",
            "stats6", "mv_ready", "std_ready", "rstd_ready", "x1_ready", "xT_psum", "xT_ready", "z_psum", "z_ready",
            "h_ready", "acc_ready", "sq_ready", "acc2_ready", "totals_sum", "bn_step",
            "bn_ready", "bn_loaded", "bn_root", "scaled", "shifted", "res_ready", "nmr_ready", "o_ready", "carry0",
            "msg_summed", "rank_step", "row_numbers", "rows_ready", "cols_psum", "same16_made", "same16_ready",
            "acc_zeroed", "negb_ready", "add_done", "place_staged",
        )}
        group_loaded = [sem(f"group_loaded{k}") for k in range(2)]
        x_loaded = [sem(f"x_loaded{k}") for k in range(X)]
        x_patched = [sem(f"x_patched{k}") for k in range(X)]
        x1_stored = [sem(f"x1_stored{k}") for k in range(X)]
        z_stored = [sem(f"z_stored{k}") for k in range(X)]
        sum0_stored = [sem(f"sum0_stored{k}") for k in range(2)]
        sum1_stored = [sem(f"sum1_stored{k}") for k in range(2)]
        rows_loaded = [sem(f"rows_loaded{k}") for k in range(4)]
        x1_back = [sem(f"x1_back{k}") for k in range(X)]
        h_patched = [sem(f"h_patched{k}") for k in range(X)]
        out_stored = [sem(f"out_stored{k}") for k in range(X)]

        def node_steps(eng, step, before, after):
            for n in range(-before, X):
                step(0, n)
            with eng.Fori(1, LAST_STEADY) as i:
                for s in range(X):
                    step(i, s)
            for n in range(LAST_STEADY * X, NT + after):
                step(0, n)

        def exists(i, j):
            return not isinstance(i, int) or 0 <= j < NT

        def tile(i, j):
            n = i * X + j
            rows = NREST if isinstance(i, int) and n == NFULL else P
            return n, j % X, i + j // X, rows

        def steady(i, n, least):
            return not isinstance(i, int) or n >= least

        def zcols(n):
            return zres[:, n * D:(n + 1) * D] if isinstance(n, int) else zres[:, bass.ds(n * D, D)]

        def col(t, n):
            return t[:, n:n + 1] if isinstance(n, int) else t[:, bass.ds(n, 1)]

        def drows(t, n, rows):
            return t[n * P:n * P + rows, :] if isinstance(n, int) else t[bass.ds(n * P, rows), :]

        def edge_steps(eng, step, ahead):
            for t in range(4 + ahead):
                step(0, t)
            with eng.Fori(1, ET // 4 - 1) as i:
                for s in range(ahead, 4 + ahead):
                    step(i, s)
            for t in range(ET - 4 + ahead, ET + ahead):
                step(0, t)

        block = es.enter_context(nc.Block())

        @block.sync
        def _(sp):
            sp.wait_ge(S["pads_ready"], 3)
            sp.dma_start(q_view(dst_q, 1, [[ET, E // ET], [1, ET]]),
                         q_view(dst, 0, [[ET, E // ET], [1, ET]])).then_inc(S["list_filled"], 16)
            sp.dma_start(q_view(src_q, 1, [[ET, E // ET], [1, ET]]),
                         q_view(src, 0, [[ET, E // ET], [1, ET]])).then_inc(S["list_filled"], 16)
            sp.dma_start(q_view(eid_q, 1, [[ET, E // ET], [1, ET]]), eid_i).then_inc(S["list_filled"], 16)
            npad = QL - E - 1
            half = npad - 128
            for a in (E + 1, E + 1 + half):
                w = half if a == E + 1 else 128
                sp.dma_start(q_view(dst_q, a, [[QL, 1], [1, w]]), pad_i[:, 0:w]).then_inc(S["list_filled"], 16)
                sp.dma_start(q_view(src_q, a, [[QL, 1], [1, w]]), zero_i[:, 0:w]).then_inc(S["list_filled"], 16)
                sp.dma_start(q_view(eid_q, a, [[QL, 1], [1, w]]), zero_i[:, 0:w]).then_inc(S["list_filled"], 16)
            sp.dma_start(q_view(dst_q, 0, [[QL, 1], [1, 1]]), zero_i[:, 0:1]).then_inc(S["list_filled"], 16)
            sp.dma_start(q_view(src_q, 0, [[QL, 1], [1, 1]]), zero_i[:, 0:1]).then_inc(S["list_filled"], 16)
            sp.dma_start(q_view(eid_q, 0, [[QL, 1], [1, 1]]), zero_i[:, 0:1]).then_inc(S["list_filled"], 16)
            sp.wait_ge(S["list_filled"], 16 * 12)
            sp.dma_start(rows_i[:, 0, :], q_view(dst_q, 0, [[EPT, ET], [1, P + 1]])).then_inc(S["first_rows"], 16)
            sp.dma_start(dst_bi, q_view(dst_q, 0, [[0, P], [1, QB]])).then_inc(S["dstb_loaded"], 16)
            sp.dma_start(wload, W.rearrange("(c o) i -> o c i", o=P)).then_inc(S["w_loaded"], 16)
            sp.dma_start(coef, q_view(coeffs, 0, [[0, P], [1, NPATH]])).then_inc(S["small_loaded"], 16)
            sp.dma_start(path_i[:, 0:3 * NPATH], q_view(paths, 0, [[3 * NPATH, 1], [1, 3 * NPATH]])).then_inc(S["small_loaded"], 16)
            sp.dma_start(negb[:], q_view(b, 0, [[0, P], [1, D]])).then_inc(S["small_loaded"], 16)
            sp.wait_ge(S["edges_final"], 1)
            sp.wait_ge(S["first_rows"], 16)
            sp.wait_ge(S["dstb_loaded"], 16)
            sp.dma_start(rows_i[:, 0, :], q_view(dst_q, 0, [[EPT, ET], [1, P + 1]])).then_inc(S["edge_rows"], 16)
            sp.dma_start(rows_i[:, 1, 0:P], q_view(src_q, 0, [[EPT, ET], [1, P]])).then_inc(S["edge_rows"], 16)
            sp.dma_start(rows_i[:, 2, 0:P], q_view(eid_q, 0, [[EPT, ET], [1, P]])).then_inc(S["edge_rows"], 16)
            sp.dma_start(dst_bi, q_view(dst_q, 0, [[0, P], [1, QB]])).then_inc(S["edge_rows"], 16)

            def store_sum(dest, stored, t, k, use):
                sp.wait_ge(S["sum_out"], t + 1)
                sp.dma_start(dest[bass.ds(t * P, P), :], ring[:, 4 + k, :]).then_inc(stored[k], 16)

            with sp.Fori(0, ET // 2) as i:
                for k in range(2):
                    store_sum(sum0, sum0_stored, 2 * i + k, k, i)
            for k in range(2):
                sp.wait_ge(sum0_stored[k], 16 * (ET // 2))

            def node_io(i, j):
                if exists(i, j + 4):
                    n, slot, use, rows = tile(i, j + 4)
                    if steady(i, n, X):
                        sp.wait_ge(x1_stored[slot], 16 * use)
                        sp.wait_ge(S["xT_psum"], n - X + 1)
                    sp.dma_start(ring[0:rows, slot, :], drows(x, n, rows)).then_inc(x_loaded[slot], 16)
                if exists(i, j + 1):
                    n, slot, use, rows = tile(i, j + 1)
                    sp.wait_ge(S["x1_ready"], n + 1)
                    sp.dma_start(drows(x1_d, n, rows), ring[0:rows, slot, :]).then_inc(x1_stored[slot], 16)
                if exists(i, j - 1):
                    n, slot, use, rows = tile(i, j - 1)
                    sp.wait_ge(S["z_ready"], n + 1)
                    sp.dma_start(drows(z_d, n, rows), zcols(n)[0:rows]).then_inc(z_stored[slot], 16)

            node_steps(sp, node_io, 4, 2)

            with sp.Fori(0, ET // 2) as i:
                for k in range(2):
                    t = 2 * i + k
                    sp.wait_ge(S["sum_out"], ET + t + 1)
                    sp.dma_start(sum1[bass.ds(t * P, P), :], ring[:, 4 + k, :]).then_inc(sum1_stored[k], 16)
            for k in range(2):
                sp.wait_ge(sum1_stored[k], 16 * (ET // 2))
            sp.wait_ge(S["z_psum"], NT)
            sp.dma_start(WT[:, 0, :], q_view(gamma, 0, [[0, P], [1, D]])).then_inc(S["bn_loaded"], 16)
            sp.dma_start(WT[:, 1, :], q_view(beta, 0, [[0, P], [1, D]])).then_inc(S["bn_loaded"], 16)
            sp.wait_ge(S["sq_ready"], NT + ET)
            sp.wait_ge(S["acc_ready"], NT + ET)

            def out_io(i, j):
                if exists(i, j + 4):
                    n, slot, use, rows = tile(i, j + 4)
                    if steady(i, n, X):
                        sp.wait_ge(out_stored[slot], 16 * use)
                    sp.dma_start(ring[0:rows, slot, :], drows(x1_d, n, rows)).then_inc(x1_back[slot], 16)
                if exists(i, j - 1):
                    n, slot, use, rows = tile(i, j - 1)
                    sp.wait_ge(S["o_ready"], n + 1)
                    sp.dma_start(drows(out, n, rows), ring[0:rows, slot, :]).then_inc(out_stored[slot], 16)

            node_steps(sp, out_io, 4, 2)
            for slot in range(X):
                sp.wait_ge(out_stored[slot], 16 * len(range(slot, NT, X)))

        @block.gpsimd
        def _(pool):
            pool.memset(ident[:], 0.0).then_inc(S["consts"], 1)
            pool.memset(ones[:], 1.0).then_inc(S["consts"], 1)
            pool.memset(pad_i, BIG).then_inc(S["pads_ready"], 1)
            pool.memset(zero_i, 0).then_inc(S["pads_ready"], 1)
            pool.iota(eid_i, pattern=[[1, ET]], base=0, channel_multiplier=ET).then_inc(S["pads_ready"], 1)
            pool.memset(epsc[:], EPS).then_inc(S["consts"], 1)
            pool.wait_ge(S["consts"], 3)
            pool.affine_select(out=ident[:], in_=ident[:], compare_op=ALU.not_equal, fill=1.0, base=0,
                               pattern=[[-1, P]], channel_multiplier=1).then_inc(S["consts"], 1)
            pool.iota(derived[:, 5, :], pattern=[[1, P]], base=1, channel_multiplier=P,
                      allow_small_or_imprecise_dtypes=True).then_inc(S["row_numbers"], 1)
            pool.iota(iota_f, pattern=[[1, P]], base=0, channel_multiplier=0,
                      allow_small_or_imprecise_dtypes=True).then_inc(S["consts"], 1)
            pool.wait_ge(S["consts"], 5)
            pool.tensor_copy(ident0[:], ident[:]).then_inc(S["consts"], 1)
            pool.wait_ge(S["consts"], 6)
            pool.memset(ident0[0:1, :], 0.0).then_inc(S["consts"], 1)

            pool.wait_ge(S["flag_ready"], 1)
            flag = pool.value_load(flag_i[0:1, 0:1], min_val=0, max_val=E)
            with pool.If(flag > 0):
                pool.memset(sort_i[:, 0, :], BIG).then_inc(S["sort_v"], 1)
                pool.memset(sort_i[:, 1, :], 0).then_inc(S["sort_v"], 1)
                pool.iota(sort_i[:, 2, :], pattern=[[1, ET]], base=0, channel_multiplier=ET).then_inc(S["sort_v"], 1)
                pool.iota(place_b, pattern=[[1, ET * P]], base=0, channel_multiplier=0,
                          allow_small_or_imprecise_dtypes=True).then_inc(S["sort_v"], 1)
                pool.wait_ge(S["sort_v"], 4)
                pool.dma_start(sort_i[0:E // ET, 0, :], q_view(dst, 0, [[ET, E // ET], [1, ET]])).then_inc(S["sort_loaded"], 16)
                pool.dma_start(sort_i[0:E // ET, 1, :], q_view(src, 0, [[ET, E // ET], [1, ET]])).then_inc(S["sort_loaded"], 16)
                pool.wait_ge(S["rank_ready"], 1)
                for t in range(ET):
                    for k, q in ((0, dst_q), (1, src_q), (2, eid_q)):
                        pool.indirect_dma_start(q, bass.IndirectOffsetOnAxis(sort_i[:, 3, t:t + 1], 0),
                                                sort_i[:, k, t:t + 1], None).then_inc(S["scattered"], 16)
                pool.wait_ge(S["scattered"], 48 * ET)
                pool.dma_start(q_view(eid_q, E + 1, [[QL, 1], [1, 120]]), zero_i[:, 0:120]).then_inc(S["sort_loaded"], 16)
                pool.wait_ge(S["sort_loaded"], 48)
            pool.sem_inc(S["edges_final"], 1)

            pool.wait_ge(S["cols_ready"], 3)
            srcc, eidc, dstc = cols_i[:, 0, :], cols_i[:, 1, :], cols_i[:, 2, :]

            def gather(dest, table, index, at, rows, done, **bounds):
                pool.indirect_dma_start(dest, None, table, bass.IndirectOffsetOnAxis(index[0:rows, at:at + 1], 0),
                                        **bounds).then_inc(done, 16)

            def load_group(g, k):
                for c in range(GT):
                    gather(x_src[k][:, c * D:(c + 1) * D], x, srcc, g * GT + c, P, group_loaded[k])
                    gather(x_edge[k][:, c * D:(c + 1) * D], edge_attr, eidc, g * GT + c, P, group_loaded[k])

            def row_tile(t, base, table, index):
                if t >= 4 or base:
                    pool.wait_ge(S["sum_done"], base + t - 3)
                gather(ring[:, t % 4, :], table, index, t, P, rows_loaded[t % 4])

            pool.wait_ge(S["tables_ready"], 1)
            load_group(0, 0)
            load_group(1, 1)
            for g in range(NG):
                for t in range(g * GT, (g + 1) * GT):
                    row_tile(t, 0, x, dstc)
                if g + 2 < NG:
                    pool.wait_ge(S["path_done"], GT * (g + 1))
                    load_group(g + 2, g % 2)

            for k in range(2):
                pool.wait_ge(sum0_stored[k], 16 * (ET // 2))

            def node_rows(i, j):
                if exists(i, j + 3):
                    n, slot, use, rows = tile(i, j + 3)
                    pool.wait_ge(x_loaded[slot], 16 * use + 16)
                    gather(ring[0:rows, slot, :], sum0, node_row, n, rows, x_patched[slot],
                           bounds_check=ET * P - 1, oob_is_err=False)
                if exists(i, j - 3):
                    n, slot, use, rows = tile(i, j - 3)
                    add_squares(n, (j - 3) % 2, rows)

            def add_squares(n, par, rows):
                pool.wait_ge(S["sq_ready"], n + 1)
                if not isinstance(n, int) or n > 0:
                    pool.wait_ge(S["acc2_ready"], n)
                pool.tensor_tensor(acc[0:rows, 1, :], acc[0:rows, 1, :], sq[0:rows, par, :],
                                   ALU.add).then_inc(S["acc2_ready"], 1)

            pool.wait_ge(S["acc_zeroed"], 2)
            for n in range(-4, NT + 3):
                node_rows(0, n)

            for slot in range(X):
                pool.wait_ge(z_stored[slot], 16 * len(range(slot, NT, X)))
                pool.wait_ge(x1_stored[slot], 16 * len(range(slot, NT, X)))
            pool.wait_ge(S["xT_psum"], NT)

            def edge_rows(_, t):
                if t < ET:
                    row_tile(t, ET, z_d, srcc)
                if t >= 3:
                    add_squares(t - 3 + NT, (t - 3 + NT) % 2, P)

            for t in range(ET + 3):
                edge_rows(0, t)

            for k in range(2):
                pool.wait_ge(sum1_stored[k], 16 * (ET // 2))

            def out_rows(i, j):
                if exists(i, j + 3):
                    n, slot, use, rows = tile(i, j + 3)
                    gather(zcols(n)[0:rows], sum1, node_row, n, rows, h_patched[slot],
                           bounds_check=ET * P - 1, oob_is_err=False)
                if exists(i, j + 1):
                    n, slot, use, rows = tile(i, j + 1)
                    pool.wait_ge(h_patched[slot], 16 * use + 16)
                    if isinstance(n, int) and n == 0:
                        pool.wait_ge(S["bn_ready"], 1)
                    pool.tensor_tensor(zcols(n)[0:rows], zcols(n)[0:rows], bn_a[0:rows],
                                       ALU.mult).then_inc(S["scaled"], 1)

            for n in range(-4, NT):
                out_rows(0, n)

        @block.tensor
        def _(pe):
            pe.wait_ge(S["prep_v"], 3)
            pe.wait_ge(S["consts"], 7)
            pe.matmul(p_misc[0:1, 0:1], flag_f[0:ET, 0:1], ones[0:ET, 0:1], start=True, stop=True).then_inc(S["flag_sum"], 1)
            pe.wait_ge(S["w_loaded"], 16)
            for k in range(KD):
                if k >= 2:
                    pe.wait_ge(S["wt_ready"], k - 1)
                for c in range(KD):
                    mm = pe.transpose(p_t[k % 2][:, c * P:(c + 1) * P], wload[:, c, k * P:(k + 1) * P], ident[:])
                mm.then_inc(S["wt_psum"], 1)
            pe.wait_ge(S["rows_ready"], 1)
            pe.wait_ge(S["flag_ready"], 1)
            lists = [rows_f[:, 0, 0:P], rows_f[:, 1, 0:P], rows_f[:, 2, 0:P]] + [derived[:, k, :] for k in range(5)]
            for k, m in enumerate(lists):
                mm = pe.transpose(p_misc[:, k * ET:(k + 1) * ET], m, ident[0:ET, 0:ET])
            mm.then_inc(S["cols_psum"], 1)
            def table_part(i, j):
                t = 2 * i + j
                pe.wait_ge(S["hot_ready"], 2 * t + 2)
                pe.matmul(p_tab[:, 0:NT], hot[:, j % 2, :], hot[:, 2 + j % 2, 0:NT], start=isinstance(t, int) and t == 0,
                          stop=isinstance(t, int) and t == ET - 1).then_inc(S["hot_used"], 1)

            for t in range(2):
                table_part(0, t)
            with pe.Fori(1, ET // 2 - 1) as i:
                for j in range(2):
                    table_part(i, j)
            for t in range(ET - 2, ET):
                table_part(0, t)

            def sum_tile(t, j, base, rows, use):
                k = j % 2
                pe.wait_ge(S["same_ready"], base + t + 1)
                if isinstance(t, int) and t == 0:
                    pe.wait_ge(S["carry0"], 2 if base else 1)
                else:
                    pe.wait_ge(S["carry_ready"], t if not base else ET - 1 + t)
                if base or not isinstance(t, int) or t >= 2:
                    pe.wait_ge(S["sum_out"], base + t - 1)
                pe.wait_ge(rows_loaded[j % 4], 16 * (base // 4 + use) + 16)
                pe.matmul(p_sum[k][:], same[:, k, :], rows, start=True, stop=bool(base)).then_inc(
                    S["sum_done" if base else "msg_summed"], 1)
                if not base:
                    pe.matmul(p_sum[k][:], ident0[:], ring[:, j % 4, :], start=False, stop=True).then_inc(S["sum_done"], 1)

            for a in range(NG // 2):
                for j in range(0 if a else 4):
                    sum_tile(j, j, 0, msg_tiles[:, j * D:(j + 1) * D], 0)
                with pe.Fori(0 if a else 1, GT // 2) as c:
                    for j in range(4):
                        sum_tile(4 * c + (2 * GT * a + j), j, 0,
                                 msg_tiles[:, bass.ds(c * (4 * D) + j * D, D)], c + 2 * GT * a // 4)

            def node_products(i, j):
                if exists(i, j + 1):
                    n, slot, use, rows = tile(i, j + 1)
                    k = (j + 1) % 2
                    pe.wait_ge(S["x1_ready"], n + 1)
                    if steady(i, n, 2):
                        pe.wait_ge(S["xT_ready"], n - 1)
                    for c in range(KD):
                        mm = pe.transpose(p_t[k][:, c * P:c * P + rows], ring[0:rows, slot, c * P:(c + 1) * P],
                                          ident[0:rows, 0:rows])
                    mm.then_inc(S["xT_psum"], 1)
                if exists(i, j):
                    n, slot, use, rows = tile(i, j)
                    k = j % 2
                    pe.wait_ge(S["xT_ready"], n + 1)
                    if steady(i, n, 2):
                        pe.wait_ge(S["z_ready"], n - 1)
                    for c in range(KD):
                        mm = pe.matmul(p_z[k][0:rows, :], xT[:, k, c, 0:rows], WT[:, c, :],
                                       start=(c == 0), stop=(c == KD - 1))
                    mm.then_inc(S["z_psum"], 1)

            node_steps(pe, node_products, 1, 0)

            def edge_sum(i, j):
                sum_tile(4 * i + j, j, ET, ring[:, j % 4, :], i + j // 4)

            edge_steps(pe, edge_sum, 0)

            pe.wait_ge(S["acc_ready"], NT + ET)
            pe.wait_ge(S["acc2_ready"], NT + ET)
            pe.matmul(p_misc[:], ones[:], acc[:, 0, :], start=True, stop=True).then_inc(S["totals_sum"], 1)
            pe.matmul(p_tab[:], ones[:], acc[:, 1, :], start=True, stop=True).then_inc(S["totals_sum"], 1)

        @block.scalar
        def _(act):
            for k in range(KD):
                act.wait_ge(S["wt_psum"], k + 1)
                act.copy(WT[:, k, :], p_t[k % 2][:]).then_inc(S["wt_ready"], 1)

            def same_matrix(t, j, base):
                if base or not isinstance(t, int) or t >= 2:
                    act.wait_ge(S["sum_done"], base + t - 1)
                act.copy(same[:, j % 2, :], same16[:, t, :] if isinstance(t, int) else same16[:, bass.ds(t, 1), :]
                         .rearrange("p a e -> p (a e)")).then_inc(S["same_ready"], 1)

            def carry(t, j, base, dest):
                act.wait_ge(S["sum_done"], base + t)
                act.copy(dest, p_sum[(j - 1) % 2][0:1, :]).then_inc(S["carry_ready"], 1)

            act.wait_ge(S["same16_ready"], 1)
            same_matrix(0, 0, 0)

            def layer0(t, j, cols):
                if not isinstance(t, int) or t > 0:
                    act.wait_ge(S["path_done"], t + 1)
                    carry(t, j, 0, cols)
                    copy_out(t - 1, j - 1)
                if not isinstance(t, int) or t + 1 < ET:
                    same_matrix(t + 1, j + 1, 0)

            def copy_out(t, j):
                k = j % 2
                if not isinstance(t, int) or t >= 2:
                    act.wait_ge(sum0_stored[k], 16 * half_of(t, j))
                act.wait_ge(S["sum_done"], t + 1)
                act.copy(ring[:, 4 + k, :], p_sum[k][:]).then_inc(S["sum_out"], 1)

            def half_of(t, j):
                return t // 2 if isinstance(t, int) else (t - j % 2) // 2

            for a in range(NG // 2):
                for j in range(0 if a else 4):
                    layer0(j, j, msg_tiles[0:1, j * D:(j + 1) * D])
                with act.Fori(0 if a else 1, GT // 2 - a) as c:
                    for j in range(4):
                        layer0(4 * c + (2 * GT * a + j), j, msg_tiles[0:1, bass.ds(c * (4 * D) + j * D, D)])
            for j in range(4):
                at = 2 * GT - 4 + j
                layer0(ET - 4 + j, j, msg_tiles[0:1, at * D:(at + 1) * D])
            copy_out(ET - 1, ET - 1)

            def node_acts(i, j):
                if exists(i, j + 1):
                    n, slot, use, rows = tile(i, j + 1)
                    k = (j + 1) % 2
                    act.wait_ge(S["xT_psum"], n + 1)
                    if steady(i, n, 2):
                        act.wait_ge(S["z_psum"], n - 1)
                    act.copy(xT[:, k, :, 0:rows], p_t[k][:].rearrange("p (c q) -> p c q", c=KD)[:, :, 0:rows]
                             ).then_inc(S["xT_ready"], 1)
                if exists(i, j + 2):
                    standard_deviation(*tile(i, j + 2), 0)
                if exists(i, j):
                    n, slot, use, rows = tile(i, j)
                    act.wait_ge(S["z_psum"], n + 1)
                    act.copy(zcols(n)[0:rows], p_z[j % 2][0:rows, :]).then_inc(S["z_ready"], 1)
                if exists(i, j - 2):
                    n, slot, use, rows = tile(i, j - 2)
                    act.wait_ge(S["h_ready"], n + 1)
                    squares(n, (j - 2) % 2, zcols(n)[0:rows], col(noedge, n)[0:rows], rows, steady(i, n, 2))

            def standard_deviation(n, slot, use, rows, done):
                act.wait_ge(S["mv_ready"], done + n + 1)
                act.activation(col(stdv, slot)[0:rows], col(mv, 2 * slot + 1)[0:rows], ACT.Sqrt,
                               bias=epsc[0:rows]).then_inc(S["std_ready"], 1)

            def squares(n, par, rows_in, mask, rows, waits):
                if waits:
                    act.wait_ge(S["acc2_ready"], n - 1)
                act.activation(sq[0:rows, par, :], rows_in, ACT.Square, scale=mask).then_inc(S["sq_ready"], 1)

            act.wait_ge(S["acc_zeroed"], 2)
            node_steps(act, node_acts, 2, 2)

            same_matrix(0, 0, ET)

            def edge_acts(i, j):
                t = 4 * i + j
                inside = not isinstance(i, int) or j < ET
                if inside and (not isinstance(i, int) or j > 0):
                    act.wait_ge(rows_loaded[j % 4], 16 * (ET // 4 + i + j // 4) + 16)
                    carry(t, j, ET, ring[0:1, j % 4, :])
                if not isinstance(i, int) or j + 1 < ET:
                    same_matrix(t + 1, j + 1, ET)
                if not isinstance(i, int) or j >= 1:
                    act.wait_ge(S["sum_out"], ET + t)
                    squares(t - 1 + NT, (j - 1 + NT) % 2, ring[:, 4 + (j - 1) % 2, :],
                            col(cols[:, 6, :], t - 1), P, True)

            edge_steps(act, edge_acts, 1)

            act.wait_ge(S["bn_step"], 4)
            act.activation(bn_t, bn_t, ACT.Sqrt, bias=epsc[:]).then_inc(S["bn_root"], 1)

            def out_acts(i, j):
                if exists(i, j + 1):
                    standard_deviation(*tile(i, j + 1), NT)
                if exists(i, j):
                    n, slot, use, rows = tile(i, j)
                    act.wait_ge(S["nmr_ready"], n + 1)
                    act.activation(ring[0:rows, slot, :], ring[0:rows, slot, :], ACT.Identity, scale=col(rstd, slot)[0:rows],
                                   bias=col(nmr, slot)[0:rows]).then_inc(S["o_ready"], 1)

            node_steps(act, out_acts, 1, 0)

        @block.vector
        def _(dve):
            count = {"prep_v": 0, "bn_step": 0}

            def link(ins, name):
                count[name] += 1
                ins.then_inc(S[name], 1)
                dve.wait_ge(S[name], count[name])

            dve.wait_ge(S["first_rows"], 16)
            link(dve.tensor_copy(rows_f[:, 0, :], rows_i[:, 0, :]), "prep_v")
            link(dve.tensor_tensor(derived[:, 0, :], rows_f[:, 0, 0:P], rows_f[:, 0, 1:P + 1], ALU.is_gt), "prep_v")
            link(dve.tensor_reduce(flag_f[0:ET, 0:1], derived[:, 0, :], AX_X, ALU.add), "prep_v")
            dve.wait_ge(S["flag_sum"], 1)
            dve.tensor_copy(flag_i[:], p_misc[0:1, 0:1]).then_inc(S["flag_ready"], 1)
            dve.wait_ge(S["flag_ready"], 1)
            flag = dve.value_load(flag_i[0:1, 0:1], min_val=0, max_val=ET * P)
            with dve.If(flag > 0):
                dve.wait_ge(S["dstb_loaded"], 16)
                dve.wait_ge(S["sort_loaded"], 32)
                dve.wait_ge(S["sort_v"], 4)
                dve.tensor_copy(dst_b, dst_bi).then_inc(S["rank_step"], 1)
                dve.tensor_copy(sort_f[:, 0, :], sort_i[:, 0, :]).then_inc(S["rank_step"], 1)
                dve.tensor_copy(sort_f[:, 1, :], sort_i[:, 2, :]).then_inc(S["rank_step"], 1)
                dve.wait_ge(S["rank_step"], 3)
                with dve.Fori(0, ET) as t:
                    dve.tensor_scalar(less_b, place_b, sort_f[:, 1, bass.ds(t, 1)], None,
                                      ALU.is_lt).then_inc(S["rank_step"], 1)
                    dve.wait_ge(S["rank_step"], 3 * t + 4)
                    dve.scalar_tensor_tensor(scr_b, dst_b[:, 1:QB], sort_f[:, 0, bass.ds(t, 1)], less_b, ALU.is_equal,
                                             ALU.mult, accum_out=sort_f[:, 2, bass.ds(t, 1)]).then_inc(S["rank_step"], 1)
                    dve.wait_ge(S["rank_step"], 3 * t + 5)
                    dve.tensor_scalar(scr_b, dst_b[:, 1:QB], sort_f[:, 0, bass.ds(t, 1)], None, ALU.is_lt, ALU.add,
                                      accum_out=sort_f[:, 3, bass.ds(t, 1)]).then_inc(S["rank_step"], 1)
                    dve.wait_ge(S["rank_step"], 3 * t + 6)
                dve.tensor_tensor(sort_f[:, 2, :], sort_f[:, 2, :], sort_f[:, 3, :], ALU.add).then_inc(S["rank_step"], 1)
                dve.wait_ge(S["rank_step"], 3 * ET + 4)
                dve.tensor_scalar(sort_i[:, 3, :], sort_f[:, 2, :], 1.0, None, ALU.add).then_inc(S["rank_ready"], 1)

            dve.wait_ge(S["edge_rows"], 16 * 4)
            dve.wait_ge(S["consts"], 7)
            dve.wait_ge(S["row_numbers"], 1)
            link(dve.tensor_copy(rows_f[:, 0, :], rows_i[:, 0, :]), "prep_v")
            dve.tensor_copy(rows_f[:, 1:3, 0:P], rows_i[:, 1:3, 0:P])
            dve.tensor_scalar(der_i[:, 0, :], rows_i[:, 0, 0:P], 7, None, ALU.arith_shift_right)
            dve.tensor_scalar(der_i[:, 1, :], rows_i[:, 0, 0:P], P - 1, None, ALU.bitwise_and)
            link(dve.tensor_tensor(derived[:, 3, :], rows_f[:, 0, 0:P], rows_f[:, 0, 1:P + 1], ALU.not_equal), "prep_v")
            link(dve.scalar_tensor_tensor(derived[:, 3, :], rows_f[:, 0, 0:P], float(BIG), derived[:, 3, :],
                                          ALU.is_lt, ALU.mult), "prep_v")
            link(dve.memset(derived[:, 3, 0:1], 0.0), "prep_v")
            dve.tensor_copy(derived[:, 0, :], der_i[:, 0, :])
            dve.tensor_copy(derived[:, 1, :], der_i[:, 1, :])
            dve.tensor_tensor(derived[:, 2, :], derived[:, 5, :], derived[:, 3, :], ALU.mult)
            dve.tensor_scalar(derived[:, 4, :], rows_f[:, 0, 0:P], float(N - 1), None, ALU.min).then_inc(S["rows_ready"], 1)
            dve.wait_ge(S["cols_psum"], 1)
            link(dve.tensor_copy(cols[:].rearrange("p a t -> p (a t)"), p_misc[:, 0:8 * ET]), "prep_v")
            dve.tensor_copy(cols_i[:, 0, :], cols[:, 1, :]).then_inc(S["cols_ready"], 1)
            dve.tensor_copy(cols_i[:, 1, :], cols[:, 2, :]).then_inc(S["cols_ready"], 1)
            dve.tensor_copy(cols_i[:, 2, :], cols[:, 7, :]).then_inc(S["cols_ready"], 1)
            link(dve.tensor_copy(dst_b, dst_bi), "prep_v")
            with dve.Fori(0, ET) as t:
                last = dve.tensor_scalar(same16[:, bass.ds(t, 1), :].rearrange("p a e -> p (a e)"),
                                         dst_b[:, bass.ds(t * EPT, P)], cols[:, 0, bass.ds(t, 1)], None, ALU.is_equal)
                last.then_inc(S["same16_made"], 1)
            dve.wait_ge(S["same16_made"], ET)
            dve.tensor_copy(same16[:, :, 0:1], same16[:, :, P - 1:P]).then_inc(S["same16_ready"], 1)
            def hot_part(i, j):
                t = 2 * i + j
                if not isinstance(t, int) or t >= 2:
                    dve.wait_ge(S["hot_used"], t - 1)
                dve.tensor_scalar(hot[:, j % 2, :], iota_f, col(cols[:, 4, :], t), None, ALU.is_equal).then_inc(S["hot_ready"], 1)
                dve.tensor_scalar(hot[:, 2 + j % 2, 0:NT], iota_f[:, 0:NT], col(cols[:, 3, :], t), col(cols[:, 5, :], t),
                                  ALU.is_equal, ALU.mult).then_inc(S["hot_ready"], 1)

            for t in range(2):
                hot_part(0, t)
            with dve.Fori(1, ET // 2) as i:
                for j in range(2):
                    hot_part(i, j)
            dve.wait_ge(S["hot_used"], ET)
            link(dve.tensor_scalar(noedge[:], p_tab[:, 0:NT], 0.0, None, ALU.is_equal), "prep_v")
            link(dve.scalar_tensor_tensor(tab_f, noedge[:], float(MISS), p_tab[:, 0:NT], ALU.mult, ALU.add), "prep_v")
            dve.tensor_scalar(node_row[:], tab_f, -1.0, None, ALU.add).then_inc(S["tables_ready"], 1)
            dve.memset(acc[:, 0, :], 0.0).then_inc(S["acc_zeroed"], 1)
            dve.memset(acc[:, 1, :], 0.0).then_inc(S["acc_zeroed"], 1)
            dve.wait_ge(S["small_loaded"], 48)
            dve.tensor_scalar(negb[:], negb[:], -1.0, None, ALU.mult).then_inc(S["negb_ready"], 1)
            link(dve.memset(path_i[:, 3 * NPATH:], 0), "prep_v")
            dve.tensor_scalar(path_i, path_i, EXT.bit_length() - 1, None, ALU.logical_shift_left).then_inc(S["path_ready"], 1)

            dve.wait_ge(S["path_ready"], 1)
            dve.wait_ge(S["wt_ready"], KD)

            def part(t, at):
                return t.rearrange("p (t d) -> p t d", d=D)[:, :, bass.ds(at, EXT)]

            segs = [[dve.alloc_register(f"seg{h}_{k}") for k in range(3 * U)] for h in range(2)]
            for g in range(NG):
                k = g % 2
                dve.wait_ge(group_loaded[k], 2 * GT * 16 * (g // 2 + 1))
                if g >= 2:
                    dve.wait_ge(S["sum_done"], GT * (g - 1))
                dve.memset(msg[k], 0.0).then_inc(S["group_zeroed"], 1)
                dve.load(segs[0], path_i[:, 0:3 * U])
                dve.wait_ge(S["group_zeroed"], g + 1)
                with dve.Fori(0, NPATH // (2 * U)) as q:
                    for h in range(2):
                        at = [dve.snap(r, min_val=0, max_val=(SEGS - 1) * EXT) for r in segs[h]]

                        def product(j):
                            dve.scalar_tensor_tensor(
                                prod[j].rearrange("p (t s) -> p t s", s=EXT), part(x_src[k], at[3 * j]),
                                coef[:, bass.ds(q * (2 * U) + (h * U + j), 1)], part(x_edge[k], at[3 * j + 1]),
                                ALU.mult, ALU.mult).then_inc(S["prod_done"], 1)

                        def add(j):
                            before = q * (2 * U) + (g * NPATH + h * U + j)
                            to = part(msg[k], at[3 * j + 2])
                            dve.wait_ge(S["prod_done"], before + 1)
                            if g or h or j:
                                dve.wait_ge(S["add_done"], before)
                            dve.tensor_tensor(to, to, prod[j].rearrange("p (t s) -> p t s", s=EXT), ALU.add
                                              ).then_inc(S["add_done"], 1)

                        product(0)
                        dve.load(segs[1 - h], path_i[:, bass.ds(q * (6 * U) + 3 * U * (h + 1), 3 * U)])
                        for j in range(1, U):
                            product(j)
                            add(j - 1)
                        add(U - 1)
                dve.wait_ge(S["add_done"], NPATH * (g + 1))
                if g == 0:
                    dve.memset(msg[0][0:1, 0:D], 0.0).then_inc(S["carry0"], 1)
                dve.sem_inc(S["path_done"], GT)

            def row_stats(rows, rin):
                dve.bn_stats(stat6[0:rows, :], rin).then_inc(S["stats6"], 1)

            def mean_variance(slot, rows):
                dve.bn_aggr(mv[0:rows, 2 * slot:2 * slot + 2], stat6[0:rows, :]).then_inc(S["mv_ready"], 1)

            def reciprocal(n, slot, rows, done):
                dve.wait_ge(S["std_ready"], done + n + 1)
                dve.reciprocal(col(rstd, slot)[0:rows], col(stdv, slot)[0:rows]).then_inc(S["rstd_ready"], 1)

            def node_vec(i, j):
                if exists(i, j + 1):
                    n, slot, use, rows = tile(i, j + 1)
                    reciprocal(n, slot, rows, 0)
                if exists(i, j + 2):
                    n, slot, use, rows = tile(i, j + 2)
                    dve.wait_ge(x_patched[slot], 16 * use + 16)
                    row_stats(rows, ring[0:rows, slot, :])
                    dve.wait_ge(S["stats6"], n + 1)
                if exists(i, j + 1):
                    n, slot, use, rows = tile(i, j + 1)
                    dve.wait_ge(S["rstd_ready"], n + 1)
                    dve.tensor_scalar(ring[0:rows, slot, :], ring[0:rows, slot, :], col(mv, 2 * slot)[0:rows], col(rstd, slot)[0:rows],
                                      ALU.subtract, ALU.mult).then_inc(S["x1_ready"], 1)
                if exists(i, j + 2):
                    n, slot, use, rows = tile(i, j + 2)
                    mean_variance(slot, rows)
                if exists(i, j - 2):
                    n, slot, use, rows = tile(i, j - 2)
                    dve.wait_ge(z_stored[slot], 16 * use + 16)
                    dve.tensor_tensor(zcols(n)[0:rows], zcols(n)[0:rows], negb[0:rows], ALU.max).then_inc(S["h_ready"], 1)
                    dve.wait_ge(S["h_ready"], n + 1)
                    add_rows(n, rows, zcols(n)[0:rows], col(noedge, n)[0:rows], steady(i, n, 1))

            def add_rows(n, rows, rows_in, mask, waits):
                if waits:
                    dve.wait_ge(S["acc_ready"], n)
                dve.scalar_tensor_tensor(acc[0:rows, 0, :], rows_in, mask, acc[0:rows, 0, :], ALU.mult,
                                         ALU.add).then_inc(S["acc_ready"], 1)

            dve.wait_ge(S["negb_ready"], 1)
            dve.wait_ge(S["acc_zeroed"], 2)
            node_steps(dve, node_vec, 2, 2)

            dve.wait_ge(rows_loaded[0], 16 * (ET // 4 + 1))
            dve.memset(ring[0:1, 0, :], 0.0).then_inc(S["carry0"], 1)

            def edge_vec(i, j):
                t = 4 * i + j
                k = j % 2
                if not isinstance(t, int) or t >= 2:
                    dve.wait_ge(sum1_stored[k], 16 * (2 * i + j // 2))
                    dve.wait_ge(S["sq_ready"], NT + t - 1)
                dve.wait_ge(S["sum_done"], ET + t + 1)
                if not isinstance(t, int) or t < ET - 1:
                    dve.wait_ge(S["carry_ready"], ET + t)
                dve.tensor_tensor(ring[:, 4 + k, :], p_sum[k][:], negb[:], ALU.max).then_inc(S["sum_out"], 1)
                dve.wait_ge(S["sum_out"], ET + t + 1)
                add_rows(NT + t, P, ring[:, 4 + k, :], col(cols[:, 6, :], t), True)

            edge_steps(dve, edge_vec, 0)

            dve.wait_ge(S["totals_sum"], 2)
            dve.wait_ge(S["bn_loaded"], 32)
            link(dve.tensor_scalar(bn_m, p_misc[:], 1.0 / N, None, ALU.mult), "bn_step")
            link(dve.tensor_tensor(acc[:, 0, :], bn_m, bn_m, ALU.mult), "bn_step")
            link(dve.tensor_scalar(bn_t, p_tab[:], 1.0 / N, None, ALU.mult), "bn_step")
            link(dve.tensor_tensor(bn_t, bn_t, acc[:, 0, :], ALU.subtract), "bn_step")
            dve.wait_ge(S["bn_root"], 1)
            link(dve.reciprocal(bn_t, bn_t), "bn_step")
            link(dve.tensor_tensor(bn_a, bn_a, bn_t, ALU.mult), "bn_step")
            S_bn = dve.tensor_tensor(bn_m, bn_m, bn_a, ALU.mult)
            link(S_bn, "bn_step")
            link(dve.tensor_tensor(bn_c, bn_c, bn_m, ALU.subtract), "bn_step")
            dve.sem_inc(S["bn_ready"], 1)

            def out_vec(i, j):
                if exists(i, j + 1):
                    n, slot, use, rows = tile(i, j + 1)
                    dve.wait_ge(x1_back[slot], 16 * use + 16)
                    dve.tensor_tensor(ring[0:rows, slot, :], ring[0:rows, slot, :], bn_c[0:rows], ALU.add).then_inc(S["shifted"], 1)
                    dve.wait_ge(S["shifted"], n + 1)
                    dve.wait_ge(S["scaled"], n + 1)
                    dve.tensor_tensor(ring[0:rows, slot, :], ring[0:rows, slot, :], zcols(n)[0:rows], ALU.add
                                      ).then_inc(S["res_ready"], 1)
                    dve.wait_ge(S["res_ready"], n + 1)
                    row_stats(rows, ring[0:rows, slot, :])
                if exists(i, j):
                    n, slot, use, rows = tile(i, j)
                    reciprocal(n, slot, rows, NT)
                if exists(i, j + 1):
                    dve.wait_ge(S["stats6"], NT + tile(i, j + 1)[0] + 1)
                if exists(i, j):
                    n, slot, use, rows = tile(i, j)
                    dve.wait_ge(S["rstd_ready"], NT + n + 1)
                    dve.scalar_tensor_tensor(col(nmr, slot)[0:rows], col(mv, 2 * slot)[0:rows], -1.0, col(rstd, slot)[0:rows],
                                             ALU.mult, ALU.mult).then_inc(S["nmr_ready"], 1)
                if exists(i, j + 1):
                    n, slot, use, rows = tile(i, j + 1)
                    mean_variance(slot, rows)

            node_steps(dve, out_vec, 1, 0)


_INS = ["x", "src", "dst", "edge_attr_512", "L0_gnn_path_coeffs", "L0_gnn_path_indices", "L1_gnn_W", "L1_gnn_b",
        "L1_gnn_gamma", "L1_gnn_beta"]


def kernel(**inputs):
    import numpy as _np
    import concourse.bacc as _bacc
    from concourse.bass_utils import run_bass_kernel_spmd as _run

    nc = _bacc.Bacc("TRN2", target_bir_lowering=False, num_devices=1)
    arrays, args = {}, []
    for name in _INS:
        a = _np.ascontiguousarray(inputs[name])
        arrays[f"in_{name}"] = a
        args.append(nc.dram_tensor(f"in_{name}", a.shape, mybir.dt.from_np(a.dtype), kind="ExternalInput").ap())
    shape = inputs["x"].shape
    args.append(nc.dram_tensor("out_0", shape, F32, kind="ExternalOutput").ap())
    build(nc, *args)
    r = _run(nc, [arrays], core_ids=[0])
    return r.results[0]["out_0"]
```

```python
from contextlib import ExitStack

import concourse.bass as bass
from concourse import mybir

F32 = mybir.dt.float32
BF16 = mybir.dt.bfloat16
I32 = mybir.dt.int32
ALU = mybir.AluOpType
ACT = mybir.ActivationFunctionType
AX_X = mybir.AxisListType.X

P = 128
EPS = 1e-5
SEGS = 16


def build(nc, x, src, dst, edge_attr, coeffs, paths, W, b, gamma, beta, out):
    N, D = x.shape
    E = src.shape[0]
    NPATH = coeffs.shape[0]
    EXT = D // SEGS
    KD = D // P
    EPT = P - 1
    ET = 40
    assert (ET - 1) * EPT < E <= ET * EPT and E % ET == 0
    QB = ET * P + 1
    E_LAST = (ET - 1) * EPT - 1
    NT = -(-N // P)
    NFULL = N // P
    NREST = N - NFULL * P
    GT = 10
    NG = ET // GT
    GW = GT * D
    X = 6
    BIG = 1 << 20
    MISS = 1 << 20
    LAST_STEADY = (NFULL // X) - 1

    es = ExitStack()
    with es:
        def sb(name, shape, dt):
            return es.enter_context(nc.sbuf_tensor(name, shape, dt))

        def sem(name):
            return es.enter_context(nc.semaphore(name))

        def dram(name, shape, dt):
            return nc.dram_tensor(name, shape, dt, kind="Internal").ap()

        src_q = dram("src_q", (QB, 1), I32)
        dst_q = dram("dst_q", (QB, 1), I32)
        eid_q = dram("eid_q", (QB, 1), I32)
        sum0 = dram("sum0", (ET * P, D), F32)
        sum1 = dram("sum1", (ET * P, D), F32)
        x1_d = dram("x1_d", (N, D), F32)
        z_d = dram("z_d", (N, D), F32)

        def q_view(t, start, steps):
            return bass.AP(t.tensor, start, steps)

        arena = sb("arena", [P, NT * D], F32)
        zres = arena
        x_src = [arena[:, k * GW:(k + 1) * GW] for k in range(2)]
        x_edge = [arena[:, (2 + k) * GW:(3 + k) * GW] for k in range(2)]
        msg = [arena[:, (4 + k) * GW:(5 + k) * GW] for k in range(2)]
        msg_tiles = arena[:, 4 * GW:6 * GW]
        w_at = 6 * GW + 16
        prod_at = w_at + KD * D
        prod = [arena[:, prod_at + k * GT * EXT:prod_at + (k + 1) * GT * EXT] for k in range(4)]
        coef_at = prod_at + 4 * GT * EXT
        coef = arena[:, coef_at:coef_at + NPATH]
        U = 8
        path_i = arena[0:1, coef_at + NPATH:coef_at + 4 * NPATH + 3 * U].bitcast(I32)
        assert coef_at + 4 * NPATH + 3 * U <= NT * D and NPATH % U == 0
        dst_bi = arena[:, 4 * GW:4 * GW + QB].bitcast(I32)
        dst_b = arena[:, 4 * GW + QB + 1:4 * GW + 2 * QB + 1]
        place_b = arena[:, 0:QB - 1]
        less_b = arena[:, QB:2 * QB - 1]
        scr_b = arena[:, 2 * QB:3 * QB - 1]
        hot_at = coef_at + 4 * NPATH + 3 * U + 4
        hot_place = arena[:, hot_at:hot_at + ET * P // 2].bitcast(BF16).rearrange("p (t e) -> p t e", t=ET)
        hot_tile = arena[:, hot_at + ET * P // 2:hot_at + ET * P // 2 + ET * NT].bitcast(BF16).rearrange(
            "p (a t n) -> p a t n", a=2, t=ET)
        assert hot_at + ET * P // 2 + ET * NT <= NT * D
        wload = arena[:, w_at:w_at + KD * D].rearrange("p (c i) -> p c i", c=KD)
        assert 4 * GW + 2 * QB + 1 <= w_at

        same16 = sb("same16", [P, ET, P], BF16)
        same = sb("same", [P, 2, P], F32)
        WT = sb("WT", [P, KD, D], F32)
        negb = sb("negb", [P, D], F32)
        acc = sb("acc", [P, 2, D], F32)
        sq = sb("sq", [P, 2, D], F32)
        ring = sb("ring", [P, X, D], F32)
        xT = sb("xT", [P, 2, KD, P], F32)
        ident = sb("ident", [P, P], F32)
        ident0 = sb("ident0", [P, P], F32)
        cols = sb("cols", [P, 9, ET], F32)
        cols_i = sb("cols_i", [P, 3, ET], I32)
        noedge = sb("noedge", [P, NT], F32)
        node_row = sb("node_row", [P, NT], I32)
        stat6 = sb("stat6", [P, 2, 6], F32)
        mv = sb("mv", [P, 2 * X], F32)
        stdv = sb("stdv", [P, X], F32)
        rstd = sb("rstd", [P, X], F32)
        nmr = sb("nmr", [P, X], F32)
        ones = sb("ones", [P, P], F32)
        epsc = sb("epsc", [P, 1], F32)
        bn_a, bn_c, bn_m, bn_t = (WT[:, k, :] for k in range(4))
        out_rows = [xT[:, k, :, :].rearrange("p c q -> p (c q)") for k in range(2)] + [bn_m, bn_t, acc[:, 0, :], acc[:, 1, :]]
        sum_rows = [ring[:, 4, :], ring[:, 5, :]] + out_rows[0:2]
        shift3 = sq[0:3, 0, 0:D // 2].bitcast(BF16)
        ones3 = sq[0:3, 1, 0:P // 2].bitcast(BF16)
        rows_i = sq[0:ET, 0, 0:3 * (P + 1)].bitcast(I32).rearrange("t (a p) -> t a p", a=3)
        rows_f = ring[0:ET, 0:3, 0:P + 1]
        derived = ring[0:ET, 3:5, :].rearrange("t a (c p) -> t (a c) p", p=P)
        der_i = xT[0:ET, 0, :, :].bitcast(I32)
        tab_f = sq[:, 0, 0:NT]
        iota_f = acc[:, 0, 0:P]
        sort_i = acc[:, 1, 0:4 * ET].bitcast(I32).rearrange("p (a t) -> p a t", a=4)
        sort_f = sq[:, 1, 0:4 * ET].rearrange("p (a t) -> p a t", a=4)
        zero_i = xT[0:1, 1, 0, 0:1].bitcast(I32)
        flag_f = sb("flag_f", [P, 2], F32)
        flag_i = sb("flag_i", [1, 1], I32)

        def bank(name):
            return es.enter_context(nc.psum_tensor(name, [P, D], F32))

        p_t = [bank("p_t0"), bank("p_t1")]
        p_z = [bank("p_z0"), bank("p_z1")]
        p_sum = [bank("p_sum0"), bank("p_sum1")]
        p_misc = bank("p_misc")
        p_tab = bank("p_tab")
        H = D // 2
        halves = [slice(0, H), slice(H, D)]

        def p_edge(j, h):
            return (p_t + p_z)[2 * (j % 2) + h][:, 0:H]

        p_out = p_t + p_z + p_sum

        S = {n: sem(n) for n in (
            "consts", "small_loaded", "w_loaded", "pads_ready", "first_rows", "dstb_loaded",
            "prep_v", "flag_sum", "flag_ready", "sort_loaded", "rank_ready", "scattered", "sort_v",
            "edges_final", "cols_ready", "hot_ready", "table_sum", "tables_ready", "wt_psum", "wt_ready",
            "same_ready", "sum_done", "carry_ready", "sum_out", "path_ready", "path_step", "path_done", "group_zeroed",
            "stats6", "mv_ready", "std_ready", "rstd_ready", "x1_ready", "xT_psum", "xT_ready", "z_psum", "z_ready",
            "h_ready", "acc_ready", "sq_ready", "sq_summed", "acc2_ready", "totals_sum", "bn_step",
            "bn_ready", "bn_loaded", "bn_root", "scaled", "res_ready", "nmr_ready", "o_ready", "carry0",
            "rank_step", "row_numbers", "rows_ready", "cols_psum", "same16_made", "same16_ready",
            "acc_zeroed", "negb_ready", "rows_v", "hot_made", "reloaded", "place_staged",
        )}
        group_loaded = [sem(f"group_loaded{k}") for k in range(2)]
        x_loaded = [sem(f"x_loaded{k}") for k in range(X)]
        x_patched = [sem(f"x_patched{k}") for k in range(X)]
        x1_stored = [sem(f"x1_stored{k}") for k in range(X)]
        z_stored = [sem(f"z_stored{k}") for k in range(X)]
        sum0_stored = [sem(f"sum0_stored{k}") for k in range(2)]
        sum1_stored = [sem(f"sum1_stored{k}") for k in range(4)]
        rows_loaded = [sem(f"rows_loaded{k}") for k in range(4)]
        x1_back = [sem(f"x1_back{k}") for k in range(X)]
        h_patched = [sem(f"h_patched{k}") for k in range(X)]
        out_stored = [sem(f"out_stored{k}") for k in range(X)]

        def node_steps(eng, step, before, after):
            for n in range(-before, X):
                step(0, n)
            with eng.Fori(1, LAST_STEADY) as i:
                for s in range(X):
                    step(i, s)
            for n in range(LAST_STEADY * X, NT + after):
                step(0, n)

        def exists(i, j):
            return not isinstance(i, int) or 0 <= j < NT

        def tile(i, j):
            n = i * X + j
            rows = NREST if isinstance(i, int) and n == NFULL else P
            return n, j % X, i + j // X, rows

        def steady(i, n, least):
            return not isinstance(i, int) or n >= least

        def zcols(n):
            return zres[:, n * D:(n + 1) * D] if isinstance(n, int) else zres[:, bass.ds(n * D, D)]

        def col(t, n):
            return t[:, n:n + 1] if isinstance(n, int) else t[:, bass.ds(n, 1)]

        def drows(t, n, rows):
            return t[n * P:n * P + rows, :] if isinstance(n, int) else t[bass.ds(n * P, rows), :]

        def edge_steps(eng, step, ahead):
            for t in range(4 + ahead):
                step(0, t)
            with eng.Fori(1, ET // 4 - 1) as i:
                for s in range(ahead, 4 + ahead):
                    step(i, s)
            for t in range(ET - 4 + ahead, ET + ahead):
                step(0, t)

        block = es.enter_context(nc.Block())

        @block.sync
        def _(sp):
            sp.wait_ge(S["pads_ready"], 7)
            for k, q, w in ((0, dst, P + 1), (1, src, P)):
                sp.dma_start(rows_i[0:1, k, 1:w], q_view(q, 0, [[E, 1], [1, w - 1]])).then_inc(S["first_rows"], 16)
                sp.dma_start(rows_i[1:ET - 1, k, 0:w], q_view(q, EPT - 1, [[EPT, ET - 2], [1, w]])).then_inc(S["first_rows"], 16)
                sp.dma_start(rows_i[ET - 1:ET, k, 0:E - E_LAST], q_view(q, E_LAST, [[E, 1], [1, E - E_LAST]])
                             ).then_inc(S["first_rows"], 16)
            sp.dma_start(wload, W.rearrange("(c o) i -> o c i", o=P)).then_inc(S["w_loaded"], 16)
            sp.dma_start(dst_bi[:, 1:E + 1], q_view(dst, 0, [[0, P], [1, E]])).then_inc(S["dstb_loaded"], 16)
            sp.dma_start(coef, q_view(coeffs, 0, [[0, P], [1, NPATH]])).then_inc(S["small_loaded"], 16)
            sp.dma_start(path_i[:, 0:3 * NPATH], q_view(paths, 0, [[3 * NPATH, 1], [1, 3 * NPATH]])).then_inc(S["small_loaded"], 16)
            sp.dma_start(negb[:], q_view(b, 0, [[0, P], [1, D]])).then_inc(S["small_loaded"], 16)

            def store_sum(dest, stored, t, k, use):
                sp.wait_ge(S["sum_out"], t + 1)
                sp.dma_start(dest[bass.ds(t * P, P), :], ring[:, 4 + k, :]).then_inc(stored[k], 16)

            with sp.Fori(0, ET // 2) as i:
                for k in range(2):
                    store_sum(sum0, sum0_stored, 2 * i + k, k, i)
            for k in range(2):
                sp.wait_ge(sum0_stored[k], 16 * (ET // 2))

            def node_io(i, j):
                if exists(i, j + 4):
                    n, slot, use, rows = tile(i, j + 4)
                    if steady(i, n, X):
                        sp.wait_ge(x1_stored[slot], 16 * use)
                        sp.wait_ge(S["xT_psum"], n - X + 1)
                    sp.dma_start(ring[0:rows, slot, :], drows(x, n, rows)).then_inc(x_loaded[slot], 16)
                if exists(i, j + 1):
                    n, slot, use, rows = tile(i, j + 1)
                    sp.wait_ge(S["x1_ready"], n + 1)
                    sp.dma_start(drows(x1_d, n, rows), ring[0:rows, slot, :]).then_inc(x1_stored[slot], 16)
                if exists(i, j - 1):
                    n, slot, use, rows = tile(i, j - 1)
                    sp.wait_ge(S["z_ready"], n + 1)
                    sp.dma_start(drows(z_d, n, rows), zcols(n)[0:rows]).then_inc(z_stored[slot], 16)

            node_steps(sp, node_io, 4, 2)

            with sp.Fori(0, ET // 4) as i:
                for k in range(4):
                    t = 4 * i + k
                    sp.wait_ge(S["sum_out"], ET + t + 1)
                    sp.dma_start(sum1[bass.ds(t * P, P), :], sum_rows[k]).then_inc(sum1_stored[k], 16)
            for k in range(4):
                sp.wait_ge(sum1_stored[k], 16 * (ET // 4))
            sp.wait_ge(S["z_psum"], NT)
            sp.dma_start(WT[:, 0, :], q_view(gamma, 0, [[0, P], [1, D]])).then_inc(S["bn_loaded"], 16)
            sp.dma_start(WT[:, 1, :], q_view(beta, 0, [[0, P], [1, D]])).then_inc(S["bn_loaded"], 16)
            sp.wait_ge(S["sq_ready"], NT + ET)
            sp.wait_ge(S["acc_ready"], NT + ET)

            def out_io(i, j):
                if exists(i, j + 4):
                    n, slot, use, rows = tile(i, j + 4)
                    if steady(i, n, X):
                        sp.wait_ge(S["res_ready"], n - X + 1)
                    sp.dma_start(ring[0:rows, slot, :], drows(x1_d, n, rows)).then_inc(x1_back[slot], 16)
                if exists(i, j):
                    n, slot, use, rows = tile(i, j)
                    sp.wait_ge(S["o_ready"], n + 1)
                    sp.dma_start(drows(out, n, rows), out_rows[slot][0:rows]).then_inc(out_stored[slot], 16)

            node_steps(sp, out_io, 4, 2)
            for slot in range(X):
                sp.wait_ge(out_stored[slot], 16 * len(range(slot, NT, X)))

        @block.gpsimd
        def _(pool):
            pool.memset(rows_i[:, 0, :], BIG).then_inc(S["pads_ready"], 1)
            pool.memset(rows_i[:, 1, :], 0).then_inc(S["pads_ready"], 1)
            pool.iota(rows_i[:, 2, 0:P], pattern=[[1, P]], base=-1, channel_multiplier=EPT).then_inc(S["pads_ready"], 1)
            pool.memset(dst_bi[:, 0:1], 0).then_inc(S["pads_ready"], 1)
            pool.memset(dst_bi[:, E + 1:QB], BIG).then_inc(S["pads_ready"], 1)
            pool.memset(zero_i, 0).then_inc(S["pads_ready"], 1)
            pool.wait_ge(S["pads_ready"], 6)
            pool.memset(rows_i[0:1, 0, 0:1], 0).then_inc(S["pads_ready"], 1)
            pool.memset(ident[:], 0.0).then_inc(S["consts"], 1)
            pool.memset(ones[:], 1.0).then_inc(S["consts"], 1)
            pool.memset(epsc[:], EPS).then_inc(S["consts"], 1)
            pool.wait_ge(S["consts"], 3)
            pool.affine_select(out=ident[:], in_=ident[:], compare_op=ALU.not_equal, fill=1.0, base=0,
                               pattern=[[-1, P]], channel_multiplier=1).then_inc(S["consts"], 1)
            pool.iota(derived[:, 6, :], pattern=[[0, P]], base=0, channel_multiplier=P,
                      allow_small_or_imprecise_dtypes=True).then_inc(S["row_numbers"], 1)
            pool.iota(derived[:, 7, :], pattern=[[1, P]], base=1, channel_multiplier=0,
                      allow_small_or_imprecise_dtypes=True).then_inc(S["row_numbers"], 1)
            pool.iota(iota_f, pattern=[[1, P]], base=0, channel_multiplier=0,
                      allow_small_or_imprecise_dtypes=True).then_inc(S["consts"], 1)
            pool.wait_ge(S["consts"], 5)
            pool.tensor_copy(ident0[:], ident[:]).then_inc(S["consts"], 1)
            pool.wait_ge(S["consts"], 6)
            pool.memset(ident0[0:1, :], 0.0).then_inc(S["consts"], 1)

            pool.wait_ge(S["flag_ready"], 1)
            flag = pool.value_load(flag_i[0:1, 0:1], min_val=0, max_val=ET * P)
            with pool.If(flag > 0):
                pool.memset(sort_i[:, 0, :], BIG).then_inc(S["sort_v"], 1)
                pool.memset(sort_i[:, 1, :], 0).then_inc(S["sort_v"], 1)
                pool.iota(sort_i[:, 2, :], pattern=[[1, ET]], base=0, channel_multiplier=ET).then_inc(S["sort_v"], 1)
                pool.iota(place_b, pattern=[[1, ET * P]], base=0, channel_multiplier=0,
                          allow_small_or_imprecise_dtypes=True).then_inc(S["sort_v"], 1)
                pool.wait_ge(S["sort_v"], 4)
                for k, q in ((0, dst), (1, src)):
                    pool.dma_start(sort_i[0:E // ET, k, :], q_view(q, 0, [[ET, E // ET], [1, ET]])).then_inc(S["sort_loaded"], 16)
                pool.wait_ge(S["rank_ready"], 1)
                for k, q in ((0, dst_q), (1, src_q), (2, eid_q)):
                    pool.dma_start(q_view(q, 0, [[QB, 1], [1, 1]]), zero_i).then_inc(S["scattered"], 16)
                    for t in range(ET):
                        pool.indirect_dma_start(q, bass.IndirectOffsetOnAxis(sort_i[:, 3, t:t + 1], 0),
                                                sort_i[:, k, t:t + 1], None).then_inc(S["scattered"], 16)
                pool.wait_ge(S["scattered"], 16 * 3 * (ET + 1))
                pool.wait_ge(S["first_rows"], 16 * 6)
                for k, q, w in ((0, dst_q, P + 1), (1, src_q, P), (2, eid_q, P)):
                    pool.dma_start(rows_i[:, k, 0:w], q_view(q, 0, [[EPT, ET], [1, w]])).then_inc(S["reloaded"], 16)
                pool.dma_start(dst_bi, q_view(dst_q, 0, [[0, P], [1, QB]])).then_inc(S["reloaded"], 16)
                pool.wait_ge(S["reloaded"], 16 * 4)
            pool.sem_inc(S["edges_final"], 1)

            pool.wait_ge(S["cols_ready"], 3)
            srcc, eidc, dstc = cols_i[:, 0, :], cols_i[:, 1, :], cols_i[:, 2, :]

            def gather(dest, table, index, at, rows, done, **bounds):
                pool.indirect_dma_start(dest, None, table, bass.IndirectOffsetOnAxis(index[0:rows, at:at + 1], 0),
                                        **bounds).then_inc(done, 16)

            def load_group(g, k):
                for c in range(GT):
                    gather(x_src[k][:, c * D:(c + 1) * D], x, srcc, g * GT + c, P, group_loaded[k])
                    gather(x_edge[k][:, c * D:(c + 1) * D], edge_attr, eidc, g * GT + c, P, group_loaded[k])

            def row_tile(t, base, table, index):
                if t >= 4 or base:
                    pool.wait_ge(S["sum_done"], 2 * (base + t - 3))
                gather(ring[:, t % 4, :], table, index, t, P, rows_loaded[t % 4])

            def zero_group(g):
                if g < 2:
                    pool.wait_ge(S["same16_made"], 1)
                else:
                    pool.wait_ge(S["sum_done"], 2 * GT * (g - 1))
                pool.memset(msg[g % 2], 0.0).then_inc(S["group_zeroed"], 1)

            load_group(0, 0)
            zero_group(0)
            load_group(1, 1)
            zero_group(1)
            pool.wait_ge(S["cols_psum"], 1)
            for g in range(NG):
                for t in range(g * GT, (g + 1) * GT):
                    row_tile(t, 0, x, dstc)
                if g + 2 < NG:
                    pool.wait_ge(S["path_done"], GT * (g + 1))
                    load_group(g + 2, g % 2)
                    zero_group(g + 2)

            pool.wait_ge(S["tables_ready"], 1)
            for k in range(2):
                pool.wait_ge(sum0_stored[k], 16 * (ET // 2))

            def node_rows(i, j):
                if exists(i, j + 3):
                    n, slot, use, rows = tile(i, j + 3)
                    pool.wait_ge(x_loaded[slot], 16 * use + 16)
                    gather(ring[0:rows, slot, :], sum0, node_row, n, rows, x_patched[slot],
                           bounds_check=ET * P - 1, oob_is_err=False)
                if exists(i, j - 3):
                    n, slot, use, rows = tile(i, j - 3)
                    add_squares(n, (j - 3) % 2, rows)

            def add_squares(n, par, rows):
                pool.wait_ge(S["sq_ready"], n + 1)
                if not isinstance(n, int) or n > 0:
                    pool.wait_ge(S["acc2_ready"], n)
                pool.tensor_tensor(acc[0:rows, 1, :], acc[0:rows, 1, :], sq[0:rows, par, :],
                                   ALU.add).then_inc(S["acc2_ready"], 1)

            pool.wait_ge(S["acc_zeroed"], 2)
            for n in range(-4, NT + 3):
                node_rows(0, n)

            for slot in range(X):
                pool.wait_ge(z_stored[slot], 16 * len(range(slot, NT, X)))
                pool.wait_ge(x1_stored[slot], 16 * len(range(slot, NT, X)))
            pool.wait_ge(S["xT_psum"], NT)

            for t in range(ET):
                row_tile(t, ET, z_d, srcc)

            for k in range(4):
                pool.wait_ge(sum1_stored[k], 16 * (ET // 4))

            for n in range(NT):
                _, slot, use, rows = tile(0, n)
                if n >= X:
                    pool.wait_ge(S["scaled"], n - X + 1)
                gather(zcols(n)[0:rows], sum1, node_row, n, rows, h_patched[slot], bounds_check=ET * P - 1, oob_is_err=False)

        @block.tensor
        def _(pe):
            pe.wait_ge(S["prep_v"], 3)
            pe.wait_ge(S["consts"], 7)
            pe.matmul(p_misc[0:1, 0:1], flag_f[0:ET, 0:1], ones[0:ET, 0:1], start=True, stop=True).then_inc(S["flag_sum"], 1)
            pe.wait_ge(S["w_loaded"], 16)
            for k in range(KD):
                if k >= 2:
                    pe.wait_ge(S["wt_ready"], k - 1)
                for c in range(KD):
                    mm = pe.transpose(p_t[k % 2][:, c * P:(c + 1) * P], wload[:, c, k * P:(k + 1) * P], ident[:])
                mm.then_inc(S["wt_psum"], 1)
            pe.wait_ge(S["rows_ready"], 1)
            pe.wait_ge(S["flag_ready"], 1)
            lists = [rows_f[:, k, 0:P] for k in range(3)] + [derived[:, k, :] for k in range(6)]
            for k, m in enumerate(lists):
                mm = pe.transpose(p_misc[:, k * ET:(k + 1) * ET], m, ident[0:ET, 0:ET])
            mm.then_inc(S["cols_psum"], 1)
            pe.wait_ge(S["hot_ready"], 2)

            def table_part(t, first, last):
                for part in range(2):
                    if isinstance(t, int):
                        place, tiles = hot_place[:, t, :], hot_tile[:, part, t, :]
                    else:
                        place = hot_place[:, bass.ds(t, 1), :].rearrange("p a e -> p (a e)")
                        tiles = hot_tile[:, part, bass.ds(t, 1), :].rearrange("p a n -> p (a n)")
                    mm = pe.matmul(p_tab[:, 0:NT], place, tiles, start=first and not part, stop=last and part == 1)
                return mm

            table_part(0, True, False)
            with pe.Fori(1, ET - 1) as t:
                table_part(t, False, False)
            table_part(ET - 1, False, True).then_inc(S["table_sum"], 1)

            def same_products(t, j, base, rows):
                pe.wait_ge(S["same_ready"], base + t + 1)
                for h in range(2):
                    if isinstance(t, int) and t == 0:
                        pe.wait_ge(S["carry0"], 2 if base else 1)
                    else:
                        pe.wait_ge(S["carry_ready"], 2 * (base + t) - 1 + h - (2 if base else 0))
                    pe.matmul(p_edge(j, h), same[:, j % 2, :], rows[h], start=bool(base), stop=True).then_inc(S["sum_done"], 1)

            def bank_free(t, base):
                if base or not isinstance(t, int) or t >= 2:
                    pe.wait_ge(S["sum_out"], base + t - 1)

            def sum_tile(t, j, rows, use):
                bank_free(t, 0)
                pe.wait_ge(rows_loaded[j % 4], 16 * use + 16)
                for h in range(2):
                    pe.matmul(p_edge(j, h), ident0[:], ring[:, j % 4, halves[h]], start=True, stop=False)
                same_products(t, j, 0, rows)

            def msg_halves(at):
                if isinstance(at, int):
                    return [msg_tiles[:, at + h * H:at + h * H + H] for h in range(2)]
                return [msg_tiles[:, bass.ds(at + h * H, H)] for h in range(2)]

            pe.wait_ge(S["wt_ready"], KD)
            for a in range(NG // 2):
                for j in range(0 if a else 4):
                    sum_tile(j, j, msg_halves(j * D), 0)
                with pe.Fori(0 if a else 1, GT // 2) as c:
                    for j in range(4):
                        sum_tile(4 * c + (2 * GT * a + j), j, msg_halves(c * (4 * D) + j * D), c + 2 * GT * a // 4)

            def node_products(i, j):
                if exists(i, j + 1):
                    n, slot, use, rows = tile(i, j + 1)
                    k = (j + 1) % 2
                    pe.wait_ge(S["x1_ready"], n + 1)
                    if steady(i, n, 2):
                        pe.wait_ge(S["xT_ready"], n - 1)
                    for c in range(KD):
                        mm = pe.transpose(p_t[k][:, c * P:c * P + rows], ring[0:rows, slot, c * P:(c + 1) * P],
                                          ident[0:rows, 0:rows])
                    mm.then_inc(S["xT_psum"], 1)
                if exists(i, j):
                    n, slot, use, rows = tile(i, j)
                    k = j % 2
                    pe.wait_ge(S["xT_ready"], n + 1)
                    if steady(i, n, 2):
                        pe.wait_ge(S["z_ready"], n - 1)
                    for c in range(KD):
                        mm = pe.matmul(p_z[k][0:rows, :], xT[:, k, c, 0:rows], WT[:, c, :],
                                       start=(c == 0), stop=(c == KD - 1))
                    mm.then_inc(S["z_psum"], 1)

            node_steps(pe, node_products, 1, 0)

            def edge_sum(i, j):
                bank_free(4 * i + j, ET)
                pe.wait_ge(rows_loaded[j % 4], 16 * (ET // 4 + i + j // 4) + 16)
                same_products(4 * i + j, j, ET, [ring[:, j % 4, halves[h]] for h in range(2)])
                if not isinstance(i, int) or j >= 3:
                    add_squares(4 * i + j - 3, j - 3)

            def add_squares(t, j):
                pe.wait_ge(S["sq_ready"], NT + t + 1)
                pe.matmul(p_tab[:], ones[:], sq[:, (NT + j) % 2, :], start=isinstance(t, int) and t == 0, stop=False
                          ).then_inc(S["sq_summed"], 1)

            pe.wait_ge(S["z_ready"], NT)
            edge_steps(pe, edge_sum, 0)
            for t in range(ET - 3, ET):
                add_squares(t, t)

            pe.wait_ge(S["acc_ready"], NT + ET)
            pe.wait_ge(S["acc2_ready"], NT)
            pe.matmul(p_misc[:], ones[:], acc[:, 0, :], start=True, stop=True).then_inc(S["totals_sum"], 1)
            pe.matmul(p_tab[:], ones[:], acc[:, 1, :], start=False, stop=True).then_inc(S["totals_sum"], 1)

            pe.wait_ge(S["bn_ready"], 1)

            def residual(i, j):
                if exists(i, j):
                    n, slot, use, rows = tile(i, j)
                    if steady(i, n, X):
                        pe.wait_ge(S["o_ready"], n - X + 1)
                    pe.wait_ge(x1_back[slot], 16 * use + 16)
                    pe.matmul(p_out[slot][0:rows, :], ident[0:rows, 0:rows], ring[0:rows, slot, :], start=True, stop=False)
                    pe.matmul(p_out[slot][0:rows, :], ones3[:, 0:rows], shift3, start=False, stop=False)
                    pe.wait_ge(S["scaled"], n + 1)
                    pe.matmul(p_out[slot][0:rows, :], ident[0:rows, 0:rows], zcols(n)[0:rows], start=False,
                              stop=True).then_inc(S["res_ready"], 1)

            node_steps(pe, residual, 0, 0)

        @block.scalar
        def _(act):
            for k in range(KD):
                act.wait_ge(S["wt_psum"], k + 1)
                act.copy(WT[:, k, :], p_t[k % 2][:]).then_inc(S["wt_ready"], 1)

            def same_matrix(t, j, base):
                if base or not isinstance(t, int) or t >= 2:
                    act.wait_ge(S["sum_done"], 2 * (base + t - 1))
                act.copy(same[:, j % 2, :], same16[:, t, :] if isinstance(t, int) else same16[:, bass.ds(t, 1), :]
                         .rearrange("p a e -> p (a e)")).then_inc(S["same_ready"], 1)

            def carry(t, j, base, dest):
                for h in range(2):
                    act.wait_ge(S["sum_done"], 2 * (base + t) - 1 + h)
                    act.copy(dest[h], p_edge(j - 1, h)[0:1, :]).then_inc(S["carry_ready"], 1)

            act.wait_ge(S["same16_ready"], 1)
            same_matrix(0, 0, 0)

            def layer0(t, j, cols):
                if not isinstance(t, int) or t > 0:
                    act.wait_ge(S["path_done"], t + 1)
                    carry(t, j, 0, cols)
                    copy_out(t - 1, j - 1)
                if not isinstance(t, int) or t + 1 < ET:
                    same_matrix(t + 1, j + 1, 0)

            def copy_out(t, j):
                k = j % 2
                if not isinstance(t, int) or t >= 2:
                    act.wait_ge(sum0_stored[k], 16 * half_of(t, j))
                act.wait_ge(S["sum_done"], 2 * (t + 1))
                act.copy(ring[:, 4 + k, halves[0]], p_edge(j, 0))
                act.copy(ring[:, 4 + k, halves[1]], p_edge(j, 1)).then_inc(S["sum_out"], 1)

            def half_of(t, j):
                return t // 2 if isinstance(t, int) else (t - j % 2) // 2

            def first_halves(at):
                if isinstance(at, int):
                    return [msg_tiles[0:1, at + h * H:at + h * H + H] for h in range(2)]
                return [msg_tiles[0:1, bass.ds(at + h * H, H)] for h in range(2)]

            for a in range(NG // 2):
                for j in range(0 if a else 4):
                    layer0(j, j, first_halves(j * D))
                with act.Fori(0 if a else 1, GT // 2 - a) as c:
                    for j in range(4):
                        layer0(4 * c + (2 * GT * a + j), j, first_halves(c * (4 * D) + j * D))
            for j in range(4):
                layer0(ET - 4 + j, j, first_halves((2 * GT - 4 + j) * D))
            copy_out(ET - 1, ET - 1)

            def node_acts(i, j):
                if exists(i, j + 1):
                    n, slot, use, rows = tile(i, j + 1)
                    k = (j + 1) % 2
                    act.wait_ge(S["xT_psum"], n + 1)
                    if steady(i, n, 2):
                        act.wait_ge(S["z_psum"], n - 1)
                    act.copy(xT[:, k, :, 0:rows], p_t[k][:].rearrange("p (c q) -> p c q", c=KD)[:, :, 0:rows]
                             ).then_inc(S["xT_ready"], 1)
                if exists(i, j + 2):
                    standard_deviation(*tile(i, j + 2), 0)
                if exists(i, j):
                    n, slot, use, rows = tile(i, j)
                    act.wait_ge(S["z_psum"], n + 1)
                    act.copy(zcols(n)[0:rows], p_z[j % 2][0:rows, :]).then_inc(S["z_ready"], 1)
                if exists(i, j - 2):
                    n, slot, use, rows = tile(i, j - 2)
                    act.wait_ge(S["h_ready"], n + 1)
                    if steady(i, n, 2):
                        act.wait_ge(S["acc2_ready"], n - 1)
                    squares(n, (j - 2) % 2, zcols(n)[0:rows], col(noedge, n)[0:rows], rows)

            def standard_deviation(n, slot, use, rows, done):
                act.wait_ge(S["mv_ready"], done + n + 1)
                act.activation(col(stdv, slot)[0:rows], col(mv, 2 * slot + 1)[0:rows], ACT.Sqrt,
                               bias=epsc[0:rows]).then_inc(S["std_ready"], 1)

            def squares(n, par, rows_in, mask, rows):
                act.activation(sq[0:rows, par, :], rows_in, ACT.Square, scale=mask).then_inc(S["sq_ready"], 1)

            act.wait_ge(S["acc_zeroed"], 2)
            node_steps(act, node_acts, 2, 2)

            same_matrix(0, 0, ET)

            def edge_acts(i, j):
                t = 4 * i + j
                if not isinstance(i, int) or 0 < j < ET:
                    act.wait_ge(rows_loaded[j % 4], 16 * (ET // 4 + i + j // 4) + 16)
                    carry(t, j, ET, [ring[0:1, j % 4, halves[h]] for h in range(2)])
                if not isinstance(i, int) or j + 1 < ET:
                    same_matrix(t + 1, j + 1, ET)
                if not isinstance(i, int) or j >= 2:
                    act.wait_ge(S["sum_out"], ET + t - 1)
                    if not isinstance(i, int) or j >= 4:
                        act.wait_ge(S["sq_summed"], t - 3)
                    else:
                        act.wait_ge(S["acc2_ready"], NT - 3 + j)
                    squares(t - 2 + NT, (j - 2 + NT) % 2, sum_rows[(j - 2) % 4], col(cols[:, 6, :], t - 2), P)

            edge_steps(act, edge_acts, 2)

            act.wait_ge(S["bn_step"], 4)
            act.activation(bn_t, bn_t, ACT.Sqrt, bias=epsc[:]).then_inc(S["bn_root"], 1)

            def out_acts(i, j):
                if exists(i, j + 1):
                    standard_deviation(*tile(i, j + 1), NT)
                if exists(i, j):
                    n, slot, use, rows = tile(i, j)
                    act.wait_ge(S["nmr_ready"], n + 1)
                    if steady(i, n, X):
                        act.wait_ge(out_stored[slot], 16 * use)
                    act.activation(out_rows[slot][0:rows], p_out[slot][0:rows, :], ACT.Identity, scale=col(rstd, slot)[0:rows],
                                   bias=col(nmr, slot)[0:rows]).then_inc(S["o_ready"], 1)

            node_steps(act, out_acts, 1, 0)

        @block.vector
        def _(dve):
            count = {"prep_v": 0, "bn_step": 0}

            def link(ins, name):
                count[name] += 1
                ins.then_inc(S[name], 1)
                dve.wait_ge(S[name], count[name])

            dve.wait_ge(S["first_rows"], 16 * 6)
            link(dve.tensor_copy(rows_f[:, 0, :], rows_i[:, 0, :]), "prep_v")
            link(dve.tensor_tensor(derived[:, 0, :], rows_f[:, 0, 0:P], rows_f[:, 0, 1:P + 1], ALU.is_gt), "prep_v")
            link(dve.tensor_reduce(flag_f[0:ET, 0:1], derived[:, 0, :], AX_X, ALU.add), "prep_v")
            dve.wait_ge(S["flag_sum"], 1)
            dve.tensor_copy(flag_i[:], p_misc[0:1, 0:1]).then_inc(S["flag_ready"], 1)
            dve.wait_ge(S["flag_ready"], 1)
            flag = dve.value_load(flag_i[0:1, 0:1], min_val=0, max_val=ET * P)
            with dve.If(flag > 0):
                dve.wait_ge(S["dstb_loaded"], 16)
                dve.wait_ge(S["sort_loaded"], 32)
                dve.wait_ge(S["sort_v"], 4)
                dve.tensor_copy(dst_b, dst_bi).then_inc(S["rank_step"], 1)
                dve.tensor_copy(sort_f[:, 0, :], sort_i[:, 0, :]).then_inc(S["rank_step"], 1)
                dve.tensor_copy(sort_f[:, 1, :], sort_i[:, 2, :]).then_inc(S["rank_step"], 1)
                dve.wait_ge(S["rank_step"], 3)
                with dve.Fori(0, ET) as t:
                    dve.tensor_scalar(less_b, place_b, sort_f[:, 1, bass.ds(t, 1)], None,
                                      ALU.is_lt).then_inc(S["rank_step"], 1)
                    dve.wait_ge(S["rank_step"], 3 * t + 4)
                    dve.scalar_tensor_tensor(scr_b, dst_b[:, 1:QB], sort_f[:, 0, bass.ds(t, 1)], less_b, ALU.is_equal,
                                             ALU.mult, accum_out=sort_f[:, 2, bass.ds(t, 1)]).then_inc(S["rank_step"], 1)
                    dve.wait_ge(S["rank_step"], 3 * t + 5)
                    dve.tensor_scalar(scr_b, dst_b[:, 1:QB], sort_f[:, 0, bass.ds(t, 1)], None, ALU.is_lt, ALU.add,
                                      accum_out=sort_f[:, 3, bass.ds(t, 1)]).then_inc(S["rank_step"], 1)
                    dve.wait_ge(S["rank_step"], 3 * t + 6)
                dve.tensor_tensor(sort_f[:, 2, :], sort_f[:, 2, :], sort_f[:, 3, :], ALU.add).then_inc(S["rank_step"], 1)
                dve.wait_ge(S["rank_step"], 3 * ET + 4)
                dve.tensor_scalar(sort_i[:, 3, :], sort_f[:, 2, :], 1.0, None, ALU.add).then_inc(S["rank_ready"], 1)

            dve.wait_ge(S["edges_final"], 1)
            dve.wait_ge(S["consts"], 7)
            dve.wait_ge(S["row_numbers"], 2)
            dve.tensor_copy(rows_f[:, 1, 0:P], rows_i[:, 1, 0:P]).then_inc(S["rows_v"], 1)
            dve.tensor_copy(rows_f[:, 2, 0:P], rows_i[:, 2, 0:P]).then_inc(S["rows_v"], 1)
            dve.tensor_copy(rows_f[:, 0, :], rows_i[:, 0, :]).then_inc(S["rows_v"], 1)
            dve.tensor_scalar(der_i[:, 0, :], rows_i[:, 0, 0:P], 7, None, ALU.arith_shift_right).then_inc(S["rows_v"], 1)
            dve.tensor_scalar(der_i[:, 1, :], rows_i[:, 0, 0:P], P - 1, None, ALU.bitwise_and).then_inc(S["rows_v"], 1)
            dve.wait_ge(S["rows_v"], 5)
            dve.tensor_scalar(rows_f[:, 2, 0:P], rows_f[:, 2, 0:P], 0.0, float(E - 1), ALU.max, ALU.min).then_inc(S["rows_v"], 1)
            dve.tensor_copy(derived[:, 0, :], der_i[:, 0, :]).then_inc(S["rows_v"], 1)
            dve.tensor_copy(derived[:, 1, :], der_i[:, 1, :]).then_inc(S["rows_v"], 1)
            dve.tensor_tensor(derived[:, 5, :], rows_f[:, 0, 0:P], rows_f[:, 0, 1:P + 1], ALU.not_equal).then_inc(S["rows_v"], 1)
            dve.tensor_scalar(derived[:, 4, :], rows_f[:, 0, 0:P], float(N - 1), None, ALU.min).then_inc(S["rows_v"], 1)
            dve.wait_ge(S["rows_v"], 9)
            dve.scalar_tensor_tensor(derived[:, 3, :], rows_f[:, 0, 0:P], float(BIG), derived[:, 5, :],
                                     ALU.is_lt, ALU.mult).then_inc(S["rows_v"], 1)
            dve.wait_ge(S["rows_v"], 11)
            dve.memset(derived[:, 3, 0:1], 0.0).then_inc(S["rows_v"], 1)
            dve.wait_ge(S["rows_v"], 12)
            dve.tensor_tensor(derived[:, 2, :], derived[:, 6, :], derived[:, 3, :], ALU.mult).then_inc(S["rows_v"], 1)
            dve.tensor_tensor(derived[:, 5, :], derived[:, 7, :], derived[:, 3, :], ALU.mult).then_inc(S["rows_v"], 1)
            dve.wait_ge(S["rows_v"], 14)
            dve.sem_inc(S["rows_ready"], 1)
            dve.wait_ge(S["dstb_loaded"], 16)
            dve.tensor_copy(dst_b, dst_bi).then_inc(S["rows_v"], 1)
            dve.wait_ge(S["cols_psum"], 1)
            link(dve.tensor_copy(cols[:].rearrange("p a t -> p (a t)"), p_misc[:, 0:9 * ET]), "prep_v")
            dve.tensor_copy(cols_i[:, 0, :], cols[:, 1, :]).then_inc(S["cols_ready"], 1)
            dve.tensor_copy(cols_i[:, 1, :], cols[:, 2, :]).then_inc(S["cols_ready"], 1)
            dve.tensor_copy(cols_i[:, 2, :], cols[:, 7, :]).then_inc(S["cols_ready"], 1)

            def over(c, n):
                return cols[:, c, :].unsqueeze(2).to_broadcast([P, ET, n])

            def lane_numbers(n):
                return iota_f[:, 0:n].unsqueeze(1).to_broadcast([P, ET, n])

            dve.wait_ge(S["rows_v"], 15)
            dst_tiles = bass.AP(dst_b.tensor, dst_b.offset, [list(dst_b.ap[0]), [EPT, ET], [1, P]])
            dve.tensor_tensor(same16[:], dst_tiles, over(0, P), ALU.is_equal).then_inc(S["same16_made"], 1)
            dve.tensor_tensor(hot_place, lane_numbers(P), over(4, P), ALU.is_equal).then_inc(S["hot_ready"], 1)
            dve.tensor_tensor(hot_tile[:, 0], lane_numbers(NT), over(3, NT), ALU.is_equal).then_inc(S["hot_made"], 1)
            dve.wait_ge(S["hot_made"], 1)
            dve.tensor_tensor(hot_tile[:, 1], hot_tile[:, 0], over(8, NT), ALU.mult).then_inc(S["hot_made"], 1)
            dve.wait_ge(S["hot_made"], 2)
            dve.tensor_tensor(hot_tile[:, 0], hot_tile[:, 0], over(5, NT), ALU.mult).then_inc(S["hot_ready"], 1)
            dve.wait_ge(S["same16_made"], 1)
            dve.tensor_copy(same16[:, :, 0:1], same16[:, :, P - 1:P]).then_inc(S["same16_ready"], 1)
            dve.wait_ge(S["hot_ready"], 2)
            dve.memset(acc[:, 0, :], 0.0).then_inc(S["acc_zeroed"], 1)
            dve.memset(acc[:, 1, :], 0.0).then_inc(S["acc_zeroed"], 1)
            dve.wait_ge(S["small_loaded"], 48)
            dve.tensor_scalar(negb[:], negb[:], -1.0, None, ALU.mult).then_inc(S["negb_ready"], 1)
            link(dve.memset(path_i[:, 3 * NPATH:], 0), "prep_v")
            dve.tensor_scalar(path_i, path_i, EXT.bit_length() - 1, None, ALU.logical_shift_left).then_inc(S["path_ready"], 1)

            dve.wait_ge(S["path_ready"], 1)
            dve.wait_ge(S["wt_ready"], KD)

            def part(t, at):
                return t.rearrange("p (t d) -> p t d", d=D)[:, :, bass.ds(at, EXT)]

            segs = [dve.alloc_register(f"seg{k}") for k in range(3 * U)]
            held_to = dve.alloc_register("held_to")
            GROUP_STEPS = 2 * NPATH + 2
            for g in range(NG):
                k = g % 2
                dve.load(segs, path_i[:, 0:3 * U])
                dve.memset(prod[(U - 1) % 4], 0.0).then_inc(S["path_step"], 1)
                dve.reg_mov(held_to, 0)
                dve.wait_ge(group_loaded[k], 2 * GT * 16 * (g // 2 + 1))
                dve.wait_ge(S["group_zeroed"], g + 1)

                def add(j, at_to, before):
                    to = part(msg[k], at_to)
                    dve.wait_ge(S["path_step"], before)
                    dve.tensor_tensor(to, to, prod[j % 4].rearrange("p (t s) -> p t s", s=EXT), ALU.add
                                      ).then_inc(S["path_step"], 1)

                with dve.Fori(0, NPATH // U) as q:
                    at = {}

                    def copy_segments(first, last):
                        for r in range(first, last):
                            at[r] = dve.snap(segs[r], min_val=0, max_val=(SEGS - 1) * EXT)

                    def product(j):
                        dve.scalar_tensor_tensor(
                            prod[j % 4].rearrange("p (t s) -> p t s", s=EXT), part(x_src[k], at[3 * j]),
                            coef[:, bass.ds(q * U + j, 1)], part(x_edge[k], at[3 * j + 1]),
                            ALU.mult, ALU.mult).then_inc(S["path_step"], 1)

                    steps = q * (2 * U) + (GROUP_STEPS * g + 1)
                    copy_segments(0, 3)
                    product(0)
                    add(U - 1, dve.snap(held_to, min_val=0, max_val=(SEGS - 1) * EXT), steps)
                    copy_segments(3, 6)
                    product(1)
                    add(0, at[2], steps + 2)
                    copy_segments(6, 3 * U)
                    dve.reg_mov(held_to, segs[3 * U - 1])
                    dve.load(segs, path_i[:, bass.ds(q * (3 * U) + 3 * U, 3 * U)])
                    for j in range(2, U):
                        product(j)
                        add(j - 1, at[3 * j - 1], steps + 2 * j)
                add(U - 1, dve.snap(held_to, min_val=0, max_val=(SEGS - 1) * EXT), GROUP_STEPS * (g + 1) - 1)
                dve.wait_ge(S["path_step"], GROUP_STEPS * (g + 1))
                if g == 1:
                    dve.wait_ge(S["table_sum"], 1)
                    link(dve.tensor_scalar(noedge[:], p_tab[:, 0:NT], 0.0, None, ALU.is_equal), "prep_v")
                    link(dve.scalar_tensor_tensor(tab_f, noedge[:], float(MISS), p_tab[:, 0:NT], ALU.mult, ALU.add), "prep_v")
                    dve.tensor_scalar(node_row[:], tab_f, -1.0, None, ALU.add).then_inc(S["tables_ready"], 1)
                if g == 0:
                    dve.memset(msg[0][0:1, 0:D], 0.0).then_inc(S["carry0"], 1)
                dve.sem_inc(S["path_done"], GT)

            def row_stats(slot, rows, rin):
                dve.bn_stats(stat6[0:rows, slot % 2, :], rin).then_inc(S["stats6"], 1)

            def mean_variance(slot, rows):
                dve.bn_aggr(mv[0:rows, 2 * slot:2 * slot + 2], stat6[0:rows, slot % 2, :]).then_inc(S["mv_ready"], 1)

            def reciprocal(n, slot, rows, done):
                dve.wait_ge(S["std_ready"], done + n + 1)
                dve.reciprocal(col(rstd, slot)[0:rows], col(stdv, slot)[0:rows]).then_inc(S["rstd_ready"], 1)

            def node_vec(i, j):
                if exists(i, j + 1):
                    n, slot, use, rows = tile(i, j + 1)
                    reciprocal(n, slot, rows, 0)
                if exists(i, j + 2):
                    n, slot, use, rows = tile(i, j + 2)
                    dve.wait_ge(x_patched[slot], 16 * use + 16)
                    row_stats(slot, rows, ring[0:rows, slot, :])
                    dve.wait_ge(S["stats6"], n + 1)
                if exists(i, j + 1):
                    n, slot, use, rows = tile(i, j + 1)
                    dve.wait_ge(S["rstd_ready"], n + 1)
                    dve.tensor_scalar(ring[0:rows, slot, :], ring[0:rows, slot, :], col(mv, 2 * slot)[0:rows], col(rstd, slot)[0:rows],
                                      ALU.subtract, ALU.mult).then_inc(S["x1_ready"], 1)
                if exists(i, j + 2):
                    n, slot, use, rows = tile(i, j + 2)
                    mean_variance(slot, rows)
                if exists(i, j - 2):
                    n, slot, use, rows = tile(i, j - 2)
                    dve.wait_ge(z_stored[slot], 16 * use + 16)
                    dve.tensor_tensor(zcols(n)[0:rows], zcols(n)[0:rows], negb[0:rows], ALU.max).then_inc(S["h_ready"], 1)
                    dve.wait_ge(S["h_ready"], n + 1)
                    add_rows(n, rows, zcols(n)[0:rows], col(noedge, n)[0:rows], steady(i, n, 1))

            def add_rows(n, rows, rows_in, mask, waits):
                if waits:
                    dve.wait_ge(S["acc_ready"], n)
                dve.scalar_tensor_tensor(acc[0:rows, 0, :], rows_in, mask, acc[0:rows, 0, :], ALU.mult,
                                         ALU.add).then_inc(S["acc_ready"], 1)

            dve.wait_ge(S["negb_ready"], 1)
            dve.wait_ge(S["acc_zeroed"], 2)
            node_steps(dve, node_vec, 2, 2)

            dve.wait_ge(rows_loaded[0], 16 * (ET // 4 + 1))
            dve.memset(ring[0:1, 0, :], 0.0).then_inc(S["carry0"], 1)

            def edge_vec(i, j):
                t = 4 * i + j
                if not isinstance(i, int) or j >= 1:
                    dve.wait_ge(S["sum_out"], ET + t)
                    add_rows(NT + t - 1, P, sum_rows[(j - 1) % 4], col(cols[:, 6, :], t - 1), True)
                if not isinstance(i, int) or j < ET:
                    if not isinstance(t, int) or t >= 4:
                        dve.wait_ge(sum1_stored[j % 4], 16 * (i + j // 4))
                        dve.wait_ge(S["sq_ready"], NT + t - 3)
                    for h in range(2):
                        dve.wait_ge(S["sum_done"], 2 * (ET + t) + 1 + h)
                        if not isinstance(t, int) or t < ET - 1:
                            dve.wait_ge(S["carry_ready"], 2 * (ET + t) - 1 + h)
                        last = dve.tensor_tensor(sum_rows[j % 4][:, halves[h]], p_edge(j, h), negb[:, halves[h]], ALU.max)
                    last.then_inc(S["sum_out"], 1)

            edge_steps(dve, edge_vec, 1)

            dve.wait_ge(S["totals_sum"], 2)
            dve.wait_ge(S["bn_loaded"], 32)
            link(dve.tensor_scalar(bn_m, p_misc[:], 1.0 / N, None, ALU.mult), "bn_step")
            link(dve.tensor_tensor(acc[:, 0, :], bn_m, bn_m, ALU.mult), "bn_step")
            link(dve.tensor_scalar(bn_t, p_tab[:], 1.0 / N, None, ALU.mult), "bn_step")
            link(dve.tensor_tensor(bn_t, bn_t, acc[:, 0, :], ALU.subtract), "bn_step")
            dve.wait_ge(S["bn_root"], 1)
            link(dve.reciprocal(bn_t, bn_t), "bn_step")
            link(dve.tensor_tensor(bn_a, bn_a, bn_t, ALU.mult), "bn_step")
            S_bn = dve.tensor_tensor(bn_m, bn_m, bn_a, ALU.mult)
            link(S_bn, "bn_step")
            link(dve.tensor_tensor(bn_c, bn_c, bn_m, ALU.subtract), "bn_step")
            parts = acc[:, 0, :].bitcast(BF16).rearrange("p (a d) -> p a d", a=2)
            third = acc[:, 1, 0:D // 2].bitcast(BF16)
            link(dve.tensor_copy(parts[0:3, 0, :], bn_c[0:3]), "bn_step")
            link(dve.tensor_tensor(bn_c[0:3], bn_c[0:3], parts[0:3, 0, :], ALU.subtract), "bn_step")
            link(dve.tensor_copy(parts[0:3, 1, :], bn_c[0:3]), "bn_step")
            link(dve.tensor_tensor(third[0:3], bn_c[0:3], parts[0:3, 1, :], ALU.subtract), "bn_step")
            link(dve.tensor_scalar(shift3, parts[0:3, 0, :], ident[0:3, 0:1], None, ALU.mult), "bn_step")
            link(dve.scalar_tensor_tensor(shift3, parts[0:3, 1, :], ident[0:3, 1:2], shift3, ALU.mult, ALU.add), "bn_step")
            link(dve.scalar_tensor_tensor(shift3, third[0:3], ident[0:3, 2:3], shift3, ALU.mult, ALU.add), "bn_step")
            link(dve.memset(ones3, 1.0), "bn_step")
            dve.sem_inc(S["bn_ready"], 1)

            def out_vec(i, j):
                if exists(i, j + 3):
                    n, slot, use, rows = tile(i, j + 3)
                    dve.wait_ge(h_patched[slot], 16 * use + 16)
                    dve.tensor_tensor(zcols(n)[0:rows], zcols(n)[0:rows], bn_a[0:rows], ALU.mult).then_inc(S["scaled"], 1)
                if exists(i, j + 1):
                    n, slot, use, rows = tile(i, j + 1)
                    dve.wait_ge(S["res_ready"], n + 1)
                    row_stats(slot, rows, p_out[slot][0:rows, :])
                if exists(i, j):
                    n, slot, use, rows = tile(i, j)
                    reciprocal(n, slot, rows, NT)
                if exists(i, j + 1):
                    dve.wait_ge(S["stats6"], NT + tile(i, j + 1)[0] + 1)
                if exists(i, j):
                    n, slot, use, rows = tile(i, j)
                    dve.wait_ge(S["rstd_ready"], NT + n + 1)
                    dve.scalar_tensor_tensor(col(nmr, slot)[0:rows], col(mv, 2 * slot)[0:rows], -1.0, col(rstd, slot)[0:rows],
                                             ALU.mult, ALU.mult).then_inc(S["nmr_ready"], 1)
                if exists(i, j + 1):
                    n, slot, use, rows = tile(i, j + 1)
                    mean_variance(slot, rows)

            node_steps(dve, out_vec, 3, 0)


_INS = ["x", "src", "dst", "edge_attr_512", "L0_gnn_path_coeffs", "L0_gnn_path_indices", "L1_gnn_W", "L1_gnn_b",
        "L1_gnn_gamma", "L1_gnn_beta"]


def kernel(**inputs):
    import numpy as _np
    import concourse.bacc as _bacc
    from concourse.bass_utils import run_bass_kernel_spmd as _run

    nc = _bacc.Bacc("TRN2", target_bir_lowering=False, num_devices=1)
    arrays, args = {}, []
    for name in _INS:
        a = _np.ascontiguousarray(inputs[name])
        arrays[f"in_{name}"] = a
        args.append(nc.dram_tensor(f"in_{name}", a.shape, mybir.dt.from_np(a.dtype), kind="ExternalInput").ap())
    shape = inputs["x"].shape
    args.append(nc.dram_tensor("out_0", shape, F32, kind="ExternalOutput").ap())
    build(nc, *args)
    r = _run(nc, [arrays], core_ids=[0])
    return r.results[0]["out_0"]
```

```python
from contextlib import ExitStack

import concourse.bass as bass
from concourse import mybir

F32 = mybir.dt.float32
F32R = mybir.dt.float32r
BF16 = mybir.dt.bfloat16
I32 = mybir.dt.int32
ALU = mybir.AluOpType
ACT = mybir.ActivationFunctionType
AX_X = mybir.AxisListType.X

P = 128
EPS = 1e-5
SEGS = 16


def build(nc, x, src, dst, edge_attr, coeffs, paths, W, b, gamma, beta, out):
    N, D = x.shape
    E = src.shape[0]
    NPATH = coeffs.shape[0]
    EXT = D // SEGS
    KD = D // P
    EPT = P - 1
    ET = 40
    assert (ET - 1) * EPT < E <= ET * EPT and E % ET == 0
    QB = ET * P + 1
    E_LAST = (ET - 1) * EPT - 1
    NT = -(-N // P)
    NFULL = N // P
    NREST = N - NFULL * P
    GT = 10
    NG = ET // GT
    GW = GT * D
    X = 6
    BIG = 1 << 20
    MISS = 1 << 20
    LAST_STEADY = (NFULL // X) - 1

    es = ExitStack()
    with es:
        def sb(name, shape, dt):
            return es.enter_context(nc.sbuf_tensor(name, shape, dt))

        def sem(name):
            return es.enter_context(nc.semaphore(name))

        def dram(name, shape, dt):
            return nc.dram_tensor(name, shape, dt, kind="Internal").ap()

        src_q = dram("src_q", (QB, 1), I32)
        dst_q = dram("dst_q", (QB, 1), I32)
        eid_q = dram("eid_q", (QB, 1), I32)
        sum0 = dram("sum0", (ET * P, D), F32)
        sum1 = dram("sum1", (ET * P, D), F32)
        same_d = dram("same_d", (P, ET * P), BF16)
        x1_d = dram("x1_d", (N, D), F32)
        z_d = dram("z_d", (N, D), F32)

        def q_view(t, start, steps):
            return bass.AP(t.tensor, start, steps)

        arena = sb("arena", [P, NT * D], F32)
        zres = arena
        x_src = [arena[:, k * GW:(k + 1) * GW] for k in range(2)]
        x_edge = [arena[:, (2 + k) * GW:(3 + k) * GW] for k in range(2)]
        msg = [arena[:, (4 + k) * GW:(5 + k) * GW] for k in range(2)]
        msg_tiles = arena[:, 4 * GW:6 * GW]
        w_at = 6 * GW + 16
        prod_at = w_at + KD * D
        prod = [arena[:, prod_at + k * GT * EXT:prod_at + (k + 1) * GT * EXT] for k in range(4)]
        coef_at = prod_at + 4 * GT * EXT
        coef = arena[:, coef_at:coef_at + NPATH]
        U = 8
        path_i = arena[0:1, coef_at + NPATH:coef_at + 4 * NPATH + 3 * U].bitcast(I32)
        assert coef_at + 4 * NPATH + 3 * U <= NT * D and NPATH % U == 0
        dst_bi = arena[:, 4 * GW:4 * GW + QB].bitcast(I32)
        dst_b = arena[:, 4 * GW + QB + 1:4 * GW + 2 * QB + 1]
        place_b = arena[:, 0:QB - 1]
        less_b = arena[:, QB:2 * QB - 1]
        scr_b = arena[:, 2 * QB:3 * QB - 1]
        hot_at = coef_at + 4 * NPATH + 3 * U + 4
        hot_place = arena[:, hot_at:hot_at + ET * P // 2].bitcast(BF16).rearrange("p (t e) -> p t e", t=ET)
        hot_tile = arena[:, hot_at + ET * P // 2:hot_at + ET * P // 2 + ET * NT].bitcast(BF16).rearrange(
            "p (a t n) -> p a t n", a=2, t=ET)
        assert hot_at + ET * P // 2 + ET * NT <= NT * D
        wload = arena[:, w_at:w_at + KD * D].rearrange("p (c i) -> p c i", c=KD)
        assert 4 * GW + 2 * QB + 1 <= w_at

        same16_at = nc.sbuf_base
        same16 = sb("same16", [P, ET, P], BF16)
        same = sb("same", [P, 2, P], F32)
        WT_at = nc.sbuf_base
        WT = sb("WT", [P, KD, D], F32)
        negb = sb("negb", [P, D], F32)
        acc = sb("acc", [P, 2, D], F32)
        sq = sb("sq", [P, 2, D], F32)
        ring = sb("ring", [P, X, D], F32)
        xT_at = nc.sbuf_base
        xT = sb("xT", [P, 2, KD, P], F32)
        W_hi = nc.alloc_sbuf_tensor_at("W_hi", [P, KD, D], F32R, offset=WT_at)
        x1_hi = nc.alloc_sbuf_tensor_at("x1_hi", [P, 2, KD, P], F32R, offset=xT_at)
        W_lo = nc.alloc_sbuf_tensor_at("W_lo", [P, KD, D], F32R, offset=same16_at)
        x1_lo = nc.alloc_sbuf_tensor_at("x1_lo", [P, KD, P], F32R, offset=same16_at + 4 * KD * D)
        assert 4 * KD * D + 4 * KD * P <= 2 * ET * P
        ident = sb("ident", [P, P], F32)
        ident0 = sb("ident0", [P, P], F32)
        cols = sb("cols", [P, 9, ET], F32)
        cols_i = sb("cols_i", [P, 3, ET], I32)
        noedge = sb("noedge", [P, NT], F32)
        node_row = sb("node_row", [P, NT], I32)
        stat6 = sb("stat6", [P, 2, 6], F32)
        mv = sb("mv", [P, 2 * X], F32)
        stdv = sb("stdv", [P, X], F32)
        rstd = sb("rstd", [P, X], F32)
        nmr = sb("nmr", [P, X], F32)
        ones = sb("ones", [P, P], F32)
        epsc = sb("epsc", [P, 1], F32)
        out_rows = [xT[:, k, :, :].rearrange("p c q -> p (c q)") for k in range(2)] + [WT[:, 2, :], WT[:, 3, :],
                                                                                      acc[:, 0, :], acc[:, 1, :]]
        bn = WT[:, 0, 0:12 * KD].rearrange("p (a c) -> p a c", c=KD)
        mean, square, var, dev, factor, shift, rest = (bn[:, k, :] for k in range(7))
        shift_parts = WT[:, 0, 12 * KD:12 * KD + 2 * KD].bitcast(BF16).rearrange("p (c a) -> p c a", a=4)
        diagonal = WT[:, 3, :].rearrange("p (c q) -> p c q", c=KD)
        ident16 = WT[:, 1, 0:P // 2].bitcast(BF16)
        ones3 = WT[0:3, 1, P // 2:P].bitcast(BF16)
        shift3 = WT[0:3, 1, P:P + D // 2].bitcast(BF16)
        bn_rows = [sq[0:1, 0, :], sq[0:1, 1, :], WT[0:1, 2, :], WT[0:1, 3, :]]
        sum_rows = [ring[:, 4, :], ring[:, 5, :]] + out_rows[0:2]
        rows_i = sq[0:ET, 0, 0:3 * (P + 1)].bitcast(I32).rearrange("t (a p) -> t a p", a=3)
        rows_f = ring[0:ET, 0:3, 0:P + 1]
        derived = ring[0:ET, 3:5, :].rearrange("t a (c p) -> t (a c) p", p=P)
        der_i = xT[0:ET, 0, :, :].bitcast(I32)
        tab_f = sq[:, 0, 0:NT]
        iota_f = acc[:, 0, 0:P]
        sort_i = acc[:, 1, 0:4 * ET].bitcast(I32).rearrange("p (a t) -> p a t", a=4)
        sort_f = sq[:, 1, 0:4 * ET].rearrange("p (a t) -> p a t", a=4)
        zero_i = xT[0:1, 1, 0, 0:1].bitcast(I32)
        flag_f = sb("flag_f", [P, 2], F32)
        flag_i = sb("flag_i", [1, 1], I32)

        def bank(name):
            return es.enter_context(nc.psum_tensor(name, [P, D], F32))

        p_t = [bank("p_t0"), bank("p_t1")]
        p_z = [bank("p_z0"), bank("p_z1")]
        p_sum = [bank("p_sum0"), bank("p_sum1")]
        p_misc = bank("p_misc")
        p_tab = bank("p_tab")
        H = D // 2
        halves = [slice(0, H), slice(H, D)]

        def p_edge(j, h):
            return (p_t + p_z)[2 * (j % 2) + h][:, 0:H]

        p_out = p_t + p_z + p_sum
        p_w = [p_misc, p_tab] + p_sum
        gamma_c, beta_c = (p_sum[0][:, k * KD:(k + 1) * KD] for k in (2, 3))

        S = {n: sem(n) for n in (
            "consts", "small_loaded", "w_loaded", "pads_ready", "first_rows", "dstb_loaded", "prep_v", "flag_sum",
            "flag_ready", "sort_loaded", "rank_ready", "scattered", "sort_v", "edges_final", "cols_ready",
            "hot_ready", "table_sum", "tables_ready", "wt_psum", "wt_ready", "same_ready", "sum_done", "carry_ready",
            "sum_out", "path_ready", "path_step", "path_done", "group_zeroed", "first_group_zeroed", "dstb_float",
            "stats6", "mv_ready", "std_ready", "rstd_ready", "x1_ready", "xT_psum", "xT_ready", "z_psum", "z_ready",
            "h_ready", "acc_ready", "sq_ready", "sq_summed", "acc2_ready", "totals_sum", "bn_step", "same_saved",
            "first_same_back", "same_back", "W_lo_ready", "x1_lo_ready", "x1_lo_used", "sum_total_out",
            "square_total_out", "totals_turned", "var_ready", "diagonal_ready", "factor_rows", "parts_ready",
            "shift_rows", "shift_ready", "bn_loaded", "bn_root", "scaled", "res_ready", "nmr_ready", "o_ready",
            "carry0", "rank_step", "row_numbers", "rows_ready", "cols_psum", "same16_made", "same16_ready",
            "acc_zeroed", "negb_ready", "rows_v", "hot_made", "reloaded",
        )}
        group_loaded = [sem(f"group_loaded{k}") for k in range(2)]
        x_loaded = [sem(f"x_loaded{k}") for k in range(X)]
        x_patched = [sem(f"x_patched{k}") for k in range(X)]
        x1_stored = [sem(f"x1_stored{k}") for k in range(X)]
        z_stored = [sem(f"z_stored{k}") for k in range(X)]
        sum0_stored = [sem(f"sum0_stored{k}") for k in range(2)]
        sum1_stored = [sem(f"sum1_stored{k}") for k in range(4)]
        rows_loaded = [sem(f"rows_loaded{k}") for k in range(4)]
        x1_back = [sem(f"x1_back{k}") for k in range(X)]
        h_patched = [sem(f"h_patched{k}") for k in range(X)]
        h_patched_early = [sem(f"h_patched_early{k}") for k in range(X)]
        out_stored = [sem(f"out_stored{k}") for k in range(X)]

        def node_steps(eng, step, before, after, first=1):
            for n in range(-before, first * X):
                step(0, n)
            with eng.Fori(first, LAST_STEADY) as i:
                for s in range(X):
                    step(i, s)
            for n in range(LAST_STEADY * X, NT + after):
                step(0, n)

        def exists(i, j):
            return not isinstance(i, int) or 0 <= j < NT

        def tile(i, j):
            n = i * X + j
            rows = NREST if isinstance(i, int) and n == NFULL else P
            return n, j % X, i + j // X, rows

        def steady(i, n, least):
            return not isinstance(i, int) or n >= least

        def zcols(n):
            return zres[:, n * D:(n + 1) * D] if isinstance(n, int) else zres[:, bass.ds(n * D, D)]

        def col(t, n):
            return t[:, n:n + 1] if isinstance(n, int) else t[:, bass.ds(n, 1)]

        def drows(t, n, rows):
            return t[n * P:n * P + rows, :] if isinstance(n, int) else t[bass.ds(n * P, rows), :]

        def edge_steps(eng, step, ahead):
            for t in range(4 + ahead):
                step(0, t)
            with eng.Fori(1, ET // 4 - 1) as i:
                for s in range(ahead, 4 + ahead):
                    step(i, s)
            for t in range(ET - 4 + ahead, ET + ahead):
                step(0, t)

        def over(c, n):
            return cols[:, c, :].unsqueeze(2).to_broadcast([P, ET, n])

        def lane_numbers(n):
            return iota_f[:, 0:n].unsqueeze(1).to_broadcast([P, ET, n])

        block = es.enter_context(nc.Block())

        @block.sync
        def _(sp):
            sp.wait_ge(S["pads_ready"], 7)
            for k, q, w in ((0, dst, P + 1), (1, src, P)):
                sp.dma_start(rows_i[0:1, k, 1:w], q_view(q, 0, [[E, 1], [1, w - 1]])).then_inc(S["first_rows"], 16)
                sp.dma_start(rows_i[1:ET - 1, k, 0:w], q_view(q, EPT - 1, [[EPT, ET - 2], [1, w]])).then_inc(S["first_rows"], 16)
                sp.dma_start(rows_i[ET - 1:ET, k, 0:E - E_LAST], q_view(q, E_LAST, [[E, 1], [1, E - E_LAST]])
                             ).then_inc(S["first_rows"], 16)
            sp.dma_start(wload, W.rearrange("(c o) i -> o c i", o=P)).then_inc(S["w_loaded"], 16)
            sp.dma_start(dst_bi[:, 1:E + 1], q_view(dst, 0, [[0, P], [1, E]])).then_inc(S["dstb_loaded"], 16)
            sp.dma_start(coef, q_view(coeffs, 0, [[0, P], [1, NPATH]])).then_inc(S["small_loaded"], 16)
            sp.dma_start(path_i[:, 0:3 * NPATH], q_view(paths, 0, [[3 * NPATH, 1], [1, 3 * NPATH]])).then_inc(S["small_loaded"], 16)
            sp.dma_start(negb[:], q_view(b, 0, [[0, P], [1, D]])).then_inc(S["small_loaded"], 16)

            sp.wait_ge(S["same16_ready"], 1)
            sp.dma_start(same_d, same16[:].rearrange("p t e -> p (t e)")).then_inc(S["same_saved"], 16)

            def store_sum(t, k):
                sp.wait_ge(S["sum_out"], t + 1)
                sp.dma_start(drows(sum0, t, P), ring[:, 4 + k, :]).then_inc(sum0_stored[k], 16)

            with sp.Fori(0, ET // 2 - 2) as i:
                for k in range(2):
                    store_sum(2 * i + k, k)
            for n in range(4):
                store_sum(ET - 4 + n, n % 2)
                sp.dma_start(ring[:, n, :], drows(x, n, P)).then_inc(x_loaded[n], 16)
            for k in range(2):
                sp.wait_ge(sum0_stored[k], 16 * (ET // 2))

            def node_io(i, j):
                if exists(i, j + 1):
                    n, slot, use, rows = tile(i, j + 1)
                    sp.wait_ge(S["x1_ready"], n + 1)
                    sp.dma_start(drows(x1_d, n, rows), ring[0:rows, slot, :]).then_inc(x1_stored[slot], 16)
                if exists(i, j - 1):
                    n, slot, use, rows = tile(i, j - 1)
                    sp.wait_ge(S["z_ready"], n + 1)
                    sp.dma_start(drows(z_d, n, rows), zcols(n)[0:rows]).then_inc(z_stored[slot], 16)
                if exists(i, j + 5):
                    n, slot, use, rows = tile(i, j + 5)
                    if steady(i, n, X):
                        sp.wait_ge(x1_stored[slot], 16 * use)
                    if steady(i, n, 4):
                        sp.dma_start(ring[0:rows, slot, :], drows(x, n, rows)).then_inc(x_loaded[slot], 16)

            node_steps(sp, node_io, 5, 2)

            sp.wait_ge(S["z_psum"], NT)
            sp.dma_start(same16[:, 0:4, :], same_d[:, 0:4 * P]).then_inc(S["first_same_back"], 16)
            sp.dma_start(bn_rows[2], q_view(gamma, 0, [[D, 1], [1, D]])).then_inc(S["bn_loaded"], 16)
            sp.dma_start(bn_rows[3], q_view(beta, 0, [[D, 1], [1, D]])).then_inc(S["bn_loaded"], 16)

            sp.dma_start(same16[:, 4:ET, :], same_d[:, 4 * P:]).then_inc(S["same_back"], 16)

            with sp.Fori(0, ET // 4) as i:
                for k in range(4):
                    t = 4 * i + k
                    sp.wait_ge(S["sum_out"], ET + t + 1)
                    sp.dma_start(sum1[bass.ds(t * P, P), :], sum_rows[k]).then_inc(sum1_stored[k], 16)
            for k in range(4):
                sp.wait_ge(sum1_stored[k], 16 * (ET // 4))
            sp.wait_ge(S["sq_ready"], NT + ET)
            sp.wait_ge(S["acc_ready"], NT + ET)

            def out_io(i, j):
                if exists(i, j + 4):
                    n, slot, use, rows = tile(i, j + 4)
                    if steady(i, n, X):
                        sp.wait_ge(S["res_ready"], n - X + 1)
                    sp.dma_start(ring[0:rows, slot, :], drows(x1_d, n, rows)).then_inc(x1_back[slot], 16)
                if exists(i, j):
                    n, slot, use, rows = tile(i, j)
                    sp.wait_ge(S["o_ready"], n + 1)
                    sp.dma_start(drows(out, n, rows), out_rows[slot][0:rows]).then_inc(out_stored[slot], 16)

            node_steps(sp, out_io, 4, 2)
            for slot in range(X):
                sp.wait_ge(out_stored[slot], 16 * len(range(slot, NT, X)))

        @block.gpsimd
        def _(pool):
            pool.memset(rows_i[:, 0, :], BIG).then_inc(S["pads_ready"], 1)
            pool.memset(rows_i[:, 1, :], 0).then_inc(S["pads_ready"], 1)
            pool.iota(rows_i[:, 2, 0:P], pattern=[[1, P]], base=-1, channel_multiplier=EPT).then_inc(S["pads_ready"], 1)
            pool.memset(dst_bi[:, 0:1], 0).then_inc(S["pads_ready"], 1)
            pool.memset(dst_bi[:, E + 1:QB], BIG).then_inc(S["pads_ready"], 1)
            pool.memset(zero_i, 0).then_inc(S["pads_ready"], 1)
            pool.wait_ge(S["pads_ready"], 6)
            pool.memset(rows_i[0:1, 0, 0:1], 0).then_inc(S["pads_ready"], 1)
            pool.memset(ident[:], 0.0).then_inc(S["consts"], 1)
            pool.memset(ones[:], 1.0).then_inc(S["consts"], 1)
            pool.memset(epsc[:], EPS).then_inc(S["consts"], 1)
            pool.wait_ge(S["consts"], 3)
            pool.affine_select(out=ident[:], in_=ident[:], compare_op=ALU.not_equal, fill=1.0, base=0,
                               pattern=[[-1, P]], channel_multiplier=1).then_inc(S["consts"], 1)
            pool.iota(derived[:, 6, :], pattern=[[0, P]], base=0, channel_multiplier=P,
                      allow_small_or_imprecise_dtypes=True).then_inc(S["row_numbers"], 1)
            pool.iota(derived[:, 7, :], pattern=[[1, P]], base=1, channel_multiplier=0,
                      allow_small_or_imprecise_dtypes=True).then_inc(S["row_numbers"], 1)
            pool.iota(iota_f, pattern=[[1, P]], base=0, channel_multiplier=0,
                      allow_small_or_imprecise_dtypes=True).then_inc(S["consts"], 1)
            pool.wait_ge(S["consts"], 5)
            pool.tensor_copy(ident0[:], ident[:]).then_inc(S["consts"], 1)
            pool.wait_ge(S["consts"], 6)
            pool.memset(ident0[0:1, :], 0.0).then_inc(S["consts"], 1)

            pool.wait_ge(S["flag_ready"], 1)
            flag = pool.value_load(flag_i[0:1, 0:1], min_val=0, max_val=ET * P)
            with pool.If(flag > 0):
                pool.memset(sort_i[:, 0, :], BIG).then_inc(S["sort_v"], 1)
                pool.memset(sort_i[:, 1, :], 0).then_inc(S["sort_v"], 1)
                pool.iota(sort_i[:, 2, :], pattern=[[1, ET]], base=0, channel_multiplier=ET).then_inc(S["sort_v"], 1)
                pool.iota(place_b, pattern=[[1, ET * P]], base=0, channel_multiplier=0,
                          allow_small_or_imprecise_dtypes=True).then_inc(S["sort_v"], 1)
                pool.wait_ge(S["sort_v"], 4)
                for k, q in ((0, dst), (1, src)):
                    pool.dma_start(sort_i[0:E // ET, k, :], q_view(q, 0, [[ET, E // ET], [1, ET]])).then_inc(S["sort_loaded"], 16)
                pool.wait_ge(S["rank_ready"], 1)
                for k, q in ((0, dst_q), (1, src_q), (2, eid_q)):
                    pool.dma_start(q_view(q, 0, [[QB, 1], [1, 1]]), zero_i).then_inc(S["scattered"], 16)
                    for t in range(ET):
                        pool.indirect_dma_start(q, bass.IndirectOffsetOnAxis(sort_i[:, 3, t:t + 1], 0),
                                                sort_i[:, k, t:t + 1], None).then_inc(S["scattered"], 16)
                pool.wait_ge(S["scattered"], 16 * 3 * (ET + 1))
                pool.wait_ge(S["first_rows"], 16 * 6)
                for k, q, w in ((0, dst_q, P + 1), (1, src_q, P), (2, eid_q, P)):
                    pool.dma_start(rows_i[:, k, 0:w], q_view(q, 0, [[EPT, ET], [1, w]])).then_inc(S["reloaded"], 16)
                pool.dma_start(dst_bi, q_view(dst_q, 0, [[0, P], [1, QB]])).then_inc(S["reloaded"], 16)
                pool.wait_ge(S["reloaded"], 16 * 4)
            pool.sem_inc(S["edges_final"], 1)

            pool.wait_ge(S["cols_ready"], 3)
            srcc, eidc, dstc = cols_i[:, 0, :], cols_i[:, 1, :], cols_i[:, 2, :]

            def gather(dest, table, index, at, rows, done, **bounds):
                pool.indirect_dma_start(dest, None, table, bass.IndirectOffsetOnAxis(index[0:rows, at:at + 1], 0),
                                        **bounds).then_inc(done, 16)

            def load_group(g, k):
                for c in range(GT):
                    gather(x_src[k][:, c * D:(c + 1) * D], x, srcc, g * GT + c, P, group_loaded[k])
                    gather(x_edge[k][:, c * D:(c + 1) * D], edge_attr, eidc, g * GT + c, P, group_loaded[k])

            def row_tile(t, base, table, index):
                if t >= 4 or base:
                    pool.wait_ge(S["sum_done"], 2 * (base + t - 3))
                gather(ring[:, t % 4, :], table, index, t, P, rows_loaded[t % 4])

            def zero_group(g):
                if g == 1:
                    pool.wait_ge(S["same16_made"], 1)
                else:
                    pool.wait_ge(S["sum_done"], 2 * GT * (g - 1))
                pool.memset(msg[g % 2], 0.0).then_inc(S["group_zeroed"], 1)

            load_group(0, 0)
            load_group(1, 1)
            zero_group(1)
            pool.wait_ge(S["cols_psum"], 1)
            for t in range(4):
                row_tile(t, 0, x, dstc)

            pool.wait_ge(S["hot_made"], 1)
            pool.tensor_tensor(hot_tile[:, 1], hot_tile[:, 0], over(8, NT), ALU.mult).then_inc(S["hot_made"], 1)
            pool.wait_ge(S["hot_made"], 2)
            pool.tensor_tensor(hot_tile[:, 0], hot_tile[:, 0], over(5, NT), ALU.mult).then_inc(S["hot_ready"], 1)
            pool.wait_ge(S["hot_ready"], 2)
            pool.memset(acc[:, 0, :], 0.0).then_inc(S["acc_zeroed"], 1)
            pool.memset(acc[:, 1, :], 0.0).then_inc(S["acc_zeroed"], 1)
            for g in range(NG):
                for t in range(g * GT if g else 4, (g + 1) * GT):
                    row_tile(t, 0, x, dstc)
                if g + 2 < NG:
                    pool.wait_ge(S["path_done"], GT * (g + 1))
                    load_group(g + 2, g % 2)
                    zero_group(g + 2)

            pool.wait_ge(S["tables_ready"], 1)
            for k in range(2):
                pool.wait_ge(sum0_stored[k], 16 * (ET // 2))

            def node_rows(i, j):
                if exists(i, j + 4):
                    n, slot, use, rows = tile(i, j + 4)
                    pool.wait_ge(x_loaded[slot], 16 * use + 16)
                    gather(ring[0:rows, slot, :], sum0, node_row, n, rows, x_patched[slot],
                           bounds_check=ET * P - 1, oob_is_err=False)
                if exists(i, j - 3):
                    n, slot, use, rows = tile(i, j - 3)
                    add_squares(n, (j - 3) % 2, rows)

            def add_squares(n, par, rows):
                pool.wait_ge(S["sq_ready"], n + 1)
                if not isinstance(n, int) or n > 0:
                    pool.wait_ge(S["acc2_ready"], n)
                pool.tensor_tensor(acc[0:rows, 1, :], acc[0:rows, 1, :], sq[0:rows, par, :],
                                   ALU.add).then_inc(S["acc2_ready"], 1)

            pool.wait_ge(S["acc_zeroed"], 2)
            for n in range(-4, NT + 3):
                node_rows(0, n)

            for slot in range(X):
                pool.wait_ge(z_stored[slot], 16 * len(range(slot, NT, X)))
                pool.wait_ge(x1_stored[slot], 16 * len(range(slot, NT, X)))
            pool.wait_ge(S["xT_psum"], NT)

            for t in range(ET):
                row_tile(t, ET, z_d, srcc)

            for k in range(4):
                pool.wait_ge(sum1_stored[k], 16 * (ET // 4))

            for n in range(NT):
                _, slot, use, rows = tile(0, n)
                if n >= 2 * X:
                    pool.wait_ge(S["scaled"], n - (2 * X if n < 3 * X else X) + 1)
                gather(zcols(n)[0:rows], sum1, node_row, n, rows, (h_patched_early if X <= n < 2 * X else h_patched)[slot],
                       bounds_check=ET * P - 1, oob_is_err=False)

        @block.tensor
        def _(pe):
            pe.wait_ge(S["prep_v"], 3)
            pe.wait_ge(S["consts"], 7)
            pe.matmul(p_misc[0:1, 0:1], flag_f[0:ET, 0:1], ones[0:ET, 0:1], start=True, stop=True).then_inc(S["flag_sum"], 1)
            pe.wait_ge(S["rows_ready"], 1)
            pe.wait_ge(S["flag_ready"], 1)
            lists = [rows_f[:, k, 0:P] for k in range(3)] + [derived[:, k, :] for k in range(6)]
            for k, m in enumerate(lists):
                mm = pe.transpose(p_misc[:, k * ET:(k + 1) * ET], m, ident[0:ET, 0:ET])
            mm.then_inc(S["cols_psum"], 1)
            pe.wait_ge(S["hot_ready"], 2)

            def table_part(t, first, last):
                for part in range(2):
                    if isinstance(t, int):
                        place, tiles = hot_place[:, t, :], hot_tile[:, part, t, :]
                    else:
                        place = hot_place[:, bass.ds(t, 1), :].rearrange("p a e -> p (a e)")
                        tiles = hot_tile[:, part, bass.ds(t, 1), :].rearrange("p a n -> p (a n)")
                    mm = pe.matmul(p_tab[:, 0:NT], place, tiles, start=first and not part, stop=last and part == 1)
                return mm

            table_part(0, True, False)
            with pe.Fori(1, ET - 1) as t:
                table_part(t, False, False)
            table_part(ET - 1, False, True).then_inc(S["table_sum"], 1)

            def same_products(t, j, base, rows):
                pe.wait_ge(S["same_ready"], base + t + 1)
                for h in range(2):
                    if isinstance(t, int) and t == 0:
                        pe.wait_ge(S["carry0"], 2 if base else 1)
                    else:
                        pe.wait_ge(S["carry_ready"], 2 * (base + t) - 1 + h - (2 if base else 0))
                    pe.matmul(p_edge(j, h), same[:, j % 2, :], rows[h], start=bool(base), stop=True).then_inc(S["sum_done"], 1)

            def bank_free(t, base):
                if base or not isinstance(t, int) or t >= 2:
                    pe.wait_ge(S["sum_out"], base + t - 1)

            def sum_tile(t, j, rows, use):
                bank_free(t, 0)
                pe.wait_ge(rows_loaded[j % 4], 16 * use + 16)
                for h in range(2):
                    pe.matmul(p_edge(j, h), ident0[:], ring[:, j % 4, halves[h]], start=True, stop=False)
                same_products(t, j, 0, rows)

            def msg_halves(at):
                if isinstance(at, int):
                    return [msg_tiles[:, at + h * H:at + h * H + H] for h in range(2)]
                return [msg_tiles[:, bass.ds(at + h * H, H)] for h in range(2)]

            for a in range(NG // 2):
                if a == 1:
                    pe.wait_ge(S["w_loaded"], 16)
                    pe.wait_ge(S["tables_ready"], 1)
                    for k in range(KD):
                        for c in range(KD):
                            mm = pe.transpose(p_w[k][:, c * P:(c + 1) * P], wload[:, c, k * P:(k + 1) * P], ident[:])
                        mm.then_inc(S["wt_psum"], 1)
                for j in range(0 if a else 4):
                    sum_tile(j, j, msg_halves(j * D), 0)
                with pe.Fori(0 if a else 1, GT // 2) as c:
                    for j in range(4):
                        sum_tile(4 * c + (2 * GT * a + j), j, msg_halves(c * (4 * D) + j * D), c + 2 * GT * a // 4)

            def node_products(i, j):
                if exists(i, j + 1):
                    n, slot, use, rows = tile(i, j + 1)
                    k = (j + 1) % 2
                    pe.wait_ge(S["x1_ready"], n + 1)
                    if steady(i, n, 2):
                        pe.wait_ge(S["x1_lo_ready"], n - 1)
                    for c in range(KD):
                        mm = pe.transpose(p_t[k][:, c * P:c * P + rows], ring[0:rows, slot, c * P:(c + 1) * P],
                                          ident[0:rows, 0:rows])
                    mm.then_inc(S["xT_psum"], 1)
                if exists(i, j):
                    n, slot, use, rows = tile(i, j)
                    k = j % 2
                    pe.wait_ge(S["xT_ready"], n + 1)
                    if steady(i, n, 2):
                        pe.wait_ge(S["z_ready"], n - 1)
                    pe.wait_ge(S["x1_lo_ready"], n + 1)
                    for c in range(KD):
                        mm = pe.matmul(p_z[k][0:rows, :], x1_lo[:, c, 0:rows], W_hi[:, c, :], start=(c == 0), stop=False)
                    mm.then_inc(S["x1_lo_used"], 1)
                    for c in range(KD):
                        pe.matmul(p_z[k][0:rows, :], x1_hi[:, k, c, 0:rows], W_hi[:, c, :], start=False, stop=False)
                        mm = pe.matmul(p_z[k][0:rows, :], x1_hi[:, k, c, 0:rows], W_lo[:, c, :], start=False,
                                       stop=(c == KD - 1))
                    mm.then_inc(S["z_psum"], 1)

            pe.wait_ge(S["W_lo_ready"], KD)
            node_steps(pe, node_products, 1, 0)

            def edge_sum(i, j):
                bank_free(4 * i + j, ET)
                pe.wait_ge(rows_loaded[j % 4], 16 * (ET // 4 + i + j // 4) + 16)
                same_products(4 * i + j, j, ET, [ring[:, j % 4, halves[h]] for h in range(2)])
                if not isinstance(i, int) or j >= 3:
                    add_squares(4 * i + j - 3, j - 3)

            def add_squares(t, j):
                pe.wait_ge(S["sq_ready"], NT + t + 1)
                pe.matmul(p_tab[:], ones[:], sq[:, (NT + j) % 2, :], start=isinstance(t, int) and t == 0, stop=False
                          ).then_inc(S["sq_summed"], 1)

            pe.wait_ge(S["z_ready"], NT)
            edge_steps(pe, edge_sum, 0)
            for t in range(ET - 3, ET):
                add_squares(t, t)

            pe.wait_ge(S["acc_ready"], NT + ET)
            pe.wait_ge(S["acc2_ready"], NT)
            pe.matmul(p_misc[:], ones[:], acc[:, 0, :], start=True, stop=True).then_inc(S["totals_sum"], 1)
            pe.matmul(p_tab[:], ones[:], acc[:, 1, :], start=False, stop=True).then_inc(S["totals_sum"], 1)

            def turn(k):
                for c in range(KD):
                    mm = pe.matmul(p_sum[0][:, k * KD + c:k * KD + c + 1], bn_rows[k][:, c * P:(c + 1) * P], ones[0:1, 0:1],
                                   start=True, stop=True)
                return mm

            pe.wait_ge(S["bn_loaded"], 32)
            turn(2)
            turn(3)
            pe.wait_ge(S["sum_total_out"], 1)
            turn(0)
            pe.wait_ge(S["square_total_out"], 1)
            turn(1).then_inc(S["totals_turned"], 1)

            def take_x1(i, j):
                n, slot, use, rows = tile(i, j)
                pe.wait_ge(x1_back[slot], 16 * use + 16)
                pe.matmul(p_out[slot][0:rows, :], ident[0:rows, 0:rows], ring[0:rows, slot, :], start=True, stop=False)

            take_x1(0, 0)
            take_x1(0, 1)
            pe.wait_ge(S["diagonal_ready"], 1)
            for c in range(KD):
                mm = pe.matmul(p_misc[:, c * P:(c + 1) * P], ones[:], diagonal[:, c, :], start=True, stop=True)
            mm.then_inc(S["factor_rows"], 1)
            take_x1(0, 2)
            pe.wait_ge(S["parts_ready"], 1)
            for c in range(KD):
                mm = pe.matmul(p_tab[0:3, c * P:(c + 1) * P], shift_parts[:, c, 0:3], ident16, start=True, stop=True)
            mm.then_inc(S["shift_rows"], 1)
            take_x1(0, 3)

            pe.wait_ge(S["shift_ready"], 1)

            def residual(i, j):
                if exists(i, j):
                    n, slot, use, rows = tile(i, j)
                    if steady(i, n, X):
                        pe.wait_ge(S["o_ready"], n - X + 1)
                    if steady(i, n, 4):
                        take_x1(i, j)
                    pe.matmul(p_out[slot][0:rows, :], ones3[:, 0:rows], shift3, start=False, stop=False)
                    pe.wait_ge(S["scaled"], n + 1)
                    pe.matmul(p_out[slot][0:rows, :], ident[0:rows, 0:rows], zcols(n)[0:rows], start=False,
                              stop=True).then_inc(S["res_ready"], 1)

            node_steps(pe, residual, 0, 0)

        @block.scalar
        def _(act):
            act.wait_ge(S["edges_final"], 1)
            act.wait_ge(S["dstb_loaded"], 16)
            act.copy(dst_b, dst_bi).then_inc(S["dstb_float"], 1)

            def same_matrix(t, j, base):
                if base or not isinstance(t, int) or t >= 2:
                    act.wait_ge(S["sum_done"], 2 * (base + t - 1))
                act.copy(same[:, j % 2, :], same16[:, t, :] if isinstance(t, int) else same16[:, bass.ds(t, 1), :]
                         .rearrange("p a e -> p (a e)")).then_inc(S["same_ready"], 1)

            def carry(t, j, base, dest):
                for h in range(2):
                    act.wait_ge(S["sum_done"], 2 * (base + t) - 1 + h)
                    act.copy(dest[h], p_edge(j - 1, h)[0:1, :]).then_inc(S["carry_ready"], 1)

            act.wait_ge(S["same16_ready"], 1)
            same_matrix(0, 0, 0)

            def layer0(t, j, cols):
                if not isinstance(t, int) or t > 0:
                    act.wait_ge(S["path_done"], t + 1)
                    carry(t, j, 0, cols)
                    copy_out(t - 1, j - 1)
                if not isinstance(t, int) or t + 1 < ET:
                    same_matrix(t + 1, j + 1, 0)

            def copy_out(t, j):
                k = j % 2
                if not isinstance(t, int) or t >= 2:
                    act.wait_ge(sum0_stored[k], 16 * half_of(t, j))
                act.wait_ge(S["sum_done"], 2 * (t + 1))
                act.copy(ring[:, 4 + k, halves[0]], p_edge(j, 0))
                act.copy(ring[:, 4 + k, halves[1]], p_edge(j, 1)).then_inc(S["sum_out"], 1)

            def half_of(t, j):
                return t // 2 if isinstance(t, int) else (t - j % 2) // 2

            def first_halves(at):
                if isinstance(at, int):
                    return [msg_tiles[0:1, at + h * H:at + h * H + H] for h in range(2)]
                return [msg_tiles[0:1, bass.ds(at + h * H, H)] for h in range(2)]

            for a in range(NG // 2):
                if a == 1:
                    for k in range(KD):
                        act.wait_ge(S["wt_psum"], k + 1)
                        act.copy(W_hi[:, k, :], p_w[k][:]).then_inc(S["wt_ready"], 1)
                for j in range(0 if a else 4):
                    layer0(j, j, first_halves(j * D))
                with act.Fori(0 if a else 1, GT // 2 - a) as c:
                    for j in range(4):
                        layer0(4 * c + (2 * GT * a + j), j, first_halves(c * (4 * D) + j * D))
            for j in range(4):
                layer0(ET - 4 + j, j, first_halves((2 * GT - 4 + j) * D))
            copy_out(ET - 1, ET - 1)

            def node_acts(i, j):
                if exists(i, j + 1):
                    n, slot, use, rows = tile(i, j + 1)
                    k = (j + 1) % 2
                    act.wait_ge(S["xT_psum"], n + 1)
                    if steady(i, n, 2):
                        act.wait_ge(S["z_psum"], n - 1)
                    act.copy(x1_hi[:, k, :, 0:rows], p_t[k][:].rearrange("p (c q) -> p c q", c=KD)[:, :, 0:rows]
                             ).then_inc(S["xT_ready"], 1)
                if exists(i, j + 2):
                    n, slot, use, rows = tile(i, j + 2)
                    act.wait_ge(S["nmr_ready"], n + 1)
                    act.activation(ring[0:rows, slot, :], ring[0:rows, slot, :], ACT.Identity, scale=col(rstd, slot)[0:rows],
                                   bias=col(nmr, slot)[0:rows]).then_inc(S["x1_ready"], 1)
                if exists(i, j + 3):
                    standard_deviation(*tile(i, j + 3), 0)
                if exists(i, j):
                    n, slot, use, rows = tile(i, j)
                    act.wait_ge(S["z_psum"], n + 1)
                    act.copy(zcols(n)[0:rows], p_z[j % 2][0:rows, :]).then_inc(S["z_ready"], 1)
                if exists(i, j - 2):
                    n, slot, use, rows = tile(i, j - 2)
                    act.wait_ge(S["h_ready"], n + 1)
                    if steady(i, n, 2):
                        act.wait_ge(S["acc2_ready"], n - 1)
                    squares(n, (j - 2) % 2, zcols(n)[0:rows], col(noedge, n)[0:rows], rows)

            def standard_deviation(n, slot, use, rows, done):
                act.wait_ge(S["mv_ready"], done + n + 1)
                act.activation(col(stdv, slot)[0:rows], col(mv, 2 * slot + 1)[0:rows], ACT.Sqrt,
                               bias=epsc[0:rows]).then_inc(S["std_ready"], 1)

            def squares(n, par, rows_in, mask, rows):
                act.activation(sq[0:rows, par, :], rows_in, ACT.Square, scale=mask).then_inc(S["sq_ready"], 1)

            act.wait_ge(S["acc_zeroed"], 2)
            node_steps(act, node_acts, 3, 2)

            act.wait_ge(S["first_same_back"], 16)
            same_matrix(0, 0, ET)

            def edge_acts(i, j):
                t = 4 * i + j
                if not isinstance(i, int) or 0 < j < ET:
                    act.wait_ge(rows_loaded[j % 4], 16 * (ET // 4 + i + j // 4) + 16)
                    carry(t, j, ET, [ring[0:1, j % 4, halves[h]] for h in range(2)])
                if isinstance(i, int) and j == 3:
                    act.wait_ge(S["same_back"], 16)
                if not isinstance(i, int) or j + 1 < ET:
                    same_matrix(t + 1, j + 1, ET)
                if not isinstance(i, int) or j >= 2:
                    act.wait_ge(S["sum_out"], ET + t - 1)
                    if not isinstance(i, int) or j >= 4:
                        act.wait_ge(S["sq_summed"], t - 3)
                    else:
                        act.wait_ge(S["acc2_ready"], NT - 3 + j)
                    squares(t - 2 + NT, (j - 2 + NT) % 2, sum_rows[(j - 2) % 4], col(cols[:, 6, :], t - 2), P)

            edge_steps(act, edge_acts, 2)

            act.wait_ge(S["totals_sum"], 1)
            act.copy(bn_rows[0], p_misc[0:1, :]).then_inc(S["sum_total_out"], 1)
            act.wait_ge(S["var_ready"], 1)
            act.activation(dev, var, ACT.Sqrt, bias=epsc[:]).then_inc(S["bn_root"], 1)
            act.wait_ge(S["shift_rows"], 1)
            act.copy(shift3, p_tab[0:3, :]).then_inc(S["shift_ready"], 1)

            def out_acts(i, j):
                if exists(i, j + 1):
                    standard_deviation(*tile(i, j + 1), NT)
                if exists(i, j):
                    n, slot, use, rows = tile(i, j)
                    act.wait_ge(S["nmr_ready"], NT + n + 1)
                    if steady(i, n, X):
                        act.wait_ge(out_stored[slot], 16 * use)
                    act.activation(out_rows[slot][0:rows], p_out[slot][0:rows, :], ACT.Identity, scale=col(rstd, slot)[0:rows],
                                   bias=col(nmr, slot)[0:rows]).then_inc(S["o_ready"], 1)

            node_steps(act, out_acts, 1, 0)

        @block.vector
        def _(dve):
            count = {"prep_v": 0, "bn_step": 0}

            def link(ins, name):
                count[name] += 1
                ins.then_inc(S[name], 1)
                dve.wait_ge(S[name], count[name])

            dve.wait_ge(S["first_rows"], 16 * 6)
            link(dve.tensor_copy(rows_f[:, 0, :], rows_i[:, 0, :]), "prep_v")
            link(dve.tensor_tensor(derived[:, 0, :], rows_f[:, 0, 0:P], rows_f[:, 0, 1:P + 1], ALU.is_gt), "prep_v")
            link(dve.tensor_reduce(flag_f[0:ET, 0:1], derived[:, 0, :], AX_X, ALU.add), "prep_v")
            dve.wait_ge(S["flag_sum"], 1)
            dve.tensor_copy(flag_i[:], p_misc[0:1, 0:1]).then_inc(S["flag_ready"], 1)
            dve.wait_ge(S["flag_ready"], 1)
            flag = dve.value_load(flag_i[0:1, 0:1], min_val=0, max_val=ET * P)
            with dve.If(flag > 0):
                dve.wait_ge(S["dstb_loaded"], 16)
                dve.wait_ge(S["sort_loaded"], 32)
                dve.wait_ge(S["sort_v"], 4)
                dve.tensor_copy(dst_b, dst_bi).then_inc(S["rank_step"], 1)
                dve.tensor_copy(sort_f[:, 0, :], sort_i[:, 0, :]).then_inc(S["rank_step"], 1)
                dve.tensor_copy(sort_f[:, 1, :], sort_i[:, 2, :]).then_inc(S["rank_step"], 1)
                dve.wait_ge(S["rank_step"], 3)
                with dve.Fori(0, ET) as t:
                    dve.tensor_scalar(less_b, place_b, sort_f[:, 1, bass.ds(t, 1)], None,
                                      ALU.is_lt).then_inc(S["rank_step"], 1)
                    dve.wait_ge(S["rank_step"], 3 * t + 4)
                    dve.scalar_tensor_tensor(scr_b, dst_b[:, 1:QB], sort_f[:, 0, bass.ds(t, 1)], less_b, ALU.is_equal,
                                             ALU.mult, accum_out=sort_f[:, 2, bass.ds(t, 1)]).then_inc(S["rank_step"], 1)
                    dve.wait_ge(S["rank_step"], 3 * t + 5)
                    dve.tensor_scalar(scr_b, dst_b[:, 1:QB], sort_f[:, 0, bass.ds(t, 1)], None, ALU.is_lt, ALU.add,
                                      accum_out=sort_f[:, 3, bass.ds(t, 1)]).then_inc(S["rank_step"], 1)
                    dve.wait_ge(S["rank_step"], 3 * t + 6)
                dve.tensor_tensor(sort_f[:, 2, :], sort_f[:, 2, :], sort_f[:, 3, :], ALU.add).then_inc(S["rank_step"], 1)
                dve.wait_ge(S["rank_step"], 3 * ET + 4)
                dve.tensor_scalar(sort_i[:, 3, :], sort_f[:, 2, :], 1.0, None, ALU.add).then_inc(S["rank_ready"], 1)

            dve.wait_ge(S["edges_final"], 1)
            dve.wait_ge(S["consts"], 7)
            dve.wait_ge(S["row_numbers"], 2)
            dve.tensor_copy(rows_f[:, 1, 0:P], rows_i[:, 1, 0:P]).then_inc(S["rows_v"], 1)
            dve.tensor_copy(rows_f[:, 2, 0:P], rows_i[:, 2, 0:P]).then_inc(S["rows_v"], 1)
            dve.tensor_copy(rows_f[:, 0, :], rows_i[:, 0, :]).then_inc(S["rows_v"], 1)
            dve.tensor_scalar(der_i[:, 0, :], rows_i[:, 0, 0:P], 7, None, ALU.arith_shift_right).then_inc(S["rows_v"], 1)
            dve.tensor_scalar(der_i[:, 1, :], rows_i[:, 0, 0:P], P - 1, None, ALU.bitwise_and).then_inc(S["rows_v"], 1)
            dve.wait_ge(S["rows_v"], 5)
            dve.tensor_scalar(rows_f[:, 2, 0:P], rows_f[:, 2, 0:P], 0.0, float(E - 1), ALU.max, ALU.min).then_inc(S["rows_v"], 1)
            dve.tensor_copy(derived[:, 0, :], der_i[:, 0, :]).then_inc(S["rows_v"], 1)
            dve.tensor_copy(derived[:, 1, :], der_i[:, 1, :]).then_inc(S["rows_v"], 1)
            dve.tensor_tensor(derived[:, 5, :], rows_f[:, 0, 0:P], rows_f[:, 0, 1:P + 1], ALU.not_equal).then_inc(S["rows_v"], 1)
            dve.tensor_scalar(derived[:, 4, :], rows_f[:, 0, 0:P], float(N - 1), None, ALU.min).then_inc(S["rows_v"], 1)
            dve.wait_ge(S["rows_v"], 9)
            dve.scalar_tensor_tensor(derived[:, 3, :], rows_f[:, 0, 0:P], float(BIG), derived[:, 5, :],
                                     ALU.is_lt, ALU.mult).then_inc(S["rows_v"], 1)
            dve.wait_ge(S["rows_v"], 11)
            dve.memset(derived[:, 3, 0:1], 0.0).then_inc(S["rows_v"], 1)
            dve.wait_ge(S["rows_v"], 12)
            dve.tensor_tensor(derived[:, 2, :], derived[:, 6, :], derived[:, 3, :], ALU.mult).then_inc(S["rows_v"], 1)
            dve.tensor_tensor(derived[:, 5, :], derived[:, 7, :], derived[:, 3, :], ALU.mult).then_inc(S["rows_v"], 1)
            dve.wait_ge(S["rows_v"], 14)
            dve.sem_inc(S["rows_ready"], 1)
            dve.wait_ge(S["cols_psum"], 1)
            link(dve.tensor_copy(cols[:].rearrange("p a t -> p (a t)"), p_misc[:, 0:9 * ET]), "prep_v")
            dve.tensor_copy(cols_i[:, 0, :], cols[:, 1, :]).then_inc(S["cols_ready"], 1)
            dve.tensor_copy(cols_i[:, 1, :], cols[:, 2, :]).then_inc(S["cols_ready"], 1)
            dve.tensor_copy(cols_i[:, 2, :], cols[:, 7, :]).then_inc(S["cols_ready"], 1)

            dve.tensor_tensor(hot_place, lane_numbers(P), over(4, P), ALU.is_equal).then_inc(S["hot_ready"], 1)
            dve.tensor_tensor(hot_tile[:, 0], lane_numbers(NT), over(3, NT), ALU.is_equal).then_inc(S["hot_made"], 1)
            dve.wait_ge(S["dstb_float"], 1)
            dst_tiles = bass.AP(dst_b.tensor, dst_b.offset, [list(dst_b.ap[0]), [EPT, ET], [1, P]])
            dve.tensor_tensor(same16[:], dst_tiles, over(0, P), ALU.is_equal).then_inc(S["same16_made"], 1)
            dve.wait_ge(S["same16_made"], 1)
            dve.tensor_copy(same16[:, :, 0:1], same16[:, :, P - 1:P]).then_inc(S["same16_ready"], 1)
            dve.memset(msg[0], 0.0).then_inc(S["first_group_zeroed"], 1)
            dve.wait_ge(S["small_loaded"], 48)
            dve.tensor_scalar(negb[:], negb[:], -1.0, None, ALU.mult).then_inc(S["negb_ready"], 1)
            link(dve.memset(path_i[:, 3 * NPATH:], 0), "prep_v")
            dve.tensor_scalar(path_i, path_i, EXT.bit_length() - 1, None, ALU.logical_shift_left).then_inc(S["path_ready"], 1)

            dve.wait_ge(S["path_ready"], 1)

            def part(t, at):
                return t.rearrange("p (t d) -> p t d", d=D)[:, :, bass.ds(at, EXT)]

            segs = [dve.alloc_register(f"seg{k}") for k in range(3 * U)]
            held_to = dve.alloc_register("held_to")
            GROUP_STEPS = 2 * NPATH + 2
            COPY_TURNS = 4
            for g in range(NG):
                k = g % 2
                dve.load(segs, path_i[:, 0:3 * U])
                dve.memset(prod[(U - 1) % 4], 0.0).then_inc(S["path_step"], 1)
                dve.reg_mov(held_to, 0)
                dve.wait_ge(group_loaded[k], 2 * GT * 16 * (g // 2 + 1))
                if g == 0:
                    dve.wait_ge(S["first_group_zeroed"], 1)
                else:
                    dve.wait_ge(S["group_zeroed"], g)

                def add(j, at_to, before):
                    to = part(msg[k], at_to)
                    dve.wait_ge(S["path_step"], before)
                    dve.tensor_tensor(to, to, prod[j % 4].rearrange("p (t s) -> p t s", s=EXT), ALU.add
                                      ).then_inc(S["path_step"], 1)

                with dve.Fori(0, NPATH // U) as q:
                    at = {}

                    def copy_segments(first, last):
                        for r in range(first, last):
                            at[r] = dve.snap(segs[r], min_val=0, max_val=(SEGS - 1) * EXT)

                    def product(j):
                        dve.scalar_tensor_tensor(
                            prod[j % 4].rearrange("p (t s) -> p t s", s=EXT), part(x_src[k], at[3 * j]),
                            coef[:, bass.ds(q * U + j, 1)], part(x_edge[k], at[3 * j + 1]),
                            ALU.mult, ALU.mult).then_inc(S["path_step"], 1)

                    steps = q * (2 * U) + (GROUP_STEPS * g + 1)
                    copy_segments(0, 3)
                    product(0)
                    add(U - 1, dve.snap(held_to, min_val=0, max_val=(SEGS - 1) * EXT), steps)
                    for j in range(1, U):
                        if j <= COPY_TURNS:
                            copy_segments(3 + (3 * U - 3) * (j - 1) // COPY_TURNS, 3 + (3 * U - 3) * j // COPY_TURNS)
                        product(j)
                        add(j - 1, at[3 * j - 1], steps + 2 * j)
                        if j == COPY_TURNS:
                            dve.reg_mov(held_to, segs[3 * U - 1])
                            dve.load(segs, path_i[:, bass.ds(q * (3 * U) + 3 * U, 3 * U)])
                add(U - 1, dve.snap(held_to, min_val=0, max_val=(SEGS - 1) * EXT), GROUP_STEPS * (g + 1) - 1)
                dve.wait_ge(S["path_step"], GROUP_STEPS * (g + 1))
                if g == 1:
                    dve.wait_ge(S["table_sum"], 1)
                    link(dve.tensor_scalar(noedge[:], p_tab[:, 0:NT], 0.0, None, ALU.is_equal), "prep_v")
                    link(dve.scalar_tensor_tensor(tab_f, noedge[:], float(MISS), p_tab[:, 0:NT], ALU.mult, ALU.add), "prep_v")
                    dve.tensor_scalar(node_row[:], tab_f, -1.0, None, ALU.add).then_inc(S["tables_ready"], 1)
                if g == 0:
                    dve.memset(msg[0][0:1, 0:D], 0.0).then_inc(S["carry0"], 1)
                dve.sem_inc(S["path_done"], GT)

            dve.wait_ge(S["same_ready"], ET)
            dve.wait_ge(S["same_saved"], 16)
            dve.wait_ge(S["wt_ready"], KD)
            for k in range(KD):
                dve.tensor_tensor(W_lo[:, k, :], p_w[k][:], W_hi[:, k, :].bitcast(F32), ALU.subtract).then_inc(S["W_lo_ready"], 1)

            def row_stats(slot, rows, rin):
                dve.bn_stats(stat6[0:rows, slot % 2, :], rin).then_inc(S["stats6"], 1)

            def mean_variance(slot, rows):
                dve.bn_aggr(mv[0:rows, 2 * slot:2 * slot + 2], stat6[0:rows, slot % 2, :]).then_inc(S["mv_ready"], 1)

            def reciprocal(n, slot, rows, done):
                dve.wait_ge(S["std_ready"], done + n + 1)
                dve.reciprocal(col(rstd, slot)[0:rows], col(stdv, slot)[0:rows]).then_inc(S["rstd_ready"], 1)

            def shift_of_mean(n, slot, rows, done):
                dve.wait_ge(S["rstd_ready"], done + n + 1)
                dve.scalar_tensor_tensor(col(nmr, slot)[0:rows], col(mv, 2 * slot)[0:rows], -1.0, col(rstd, slot)[0:rows],
                                         ALU.mult, ALU.mult).then_inc(S["nmr_ready"], 1)

            def node_vec(i, j):
                if exists(i, j):
                    n, slot, use, rows = tile(i, j)
                    k = j % 2
                    dve.wait_ge(S["xT_ready"], n + 1)
                    if steady(i, n, 1):
                        dve.wait_ge(S["x1_lo_used"], n)
                    dve.tensor_tensor(x1_lo[:, :, 0:rows], p_t[k][:].rearrange("p (c q) -> p c q", c=KD)[:, :, 0:rows],
                                      x1_hi[:, k, :, 0:rows].bitcast(F32), ALU.subtract).then_inc(S["x1_lo_ready"], 1)
                if exists(i, j + 2):
                    n, slot, use, rows = tile(i, j + 2)
                    reciprocal(n, slot, rows, 0)
                if exists(i, j + 2):
                    n, slot, use, rows = tile(i, j + 2)
                    shift_of_mean(n, slot, rows, 0)
                if exists(i, j - 2):
                    n, slot, use, rows = tile(i, j - 2)
                    dve.wait_ge(z_stored[slot], 16 * use + 16)
                    dve.tensor_tensor(zcols(n)[0:rows], zcols(n)[0:rows], negb[0:rows], ALU.max).then_inc(S["h_ready"], 1)
                if exists(i, j + 3):
                    n, slot, use, rows = tile(i, j + 3)
                    dve.wait_ge(x_patched[slot], 16 * use + 16)
                    row_stats(slot, rows, ring[0:rows, slot, :])
                    dve.wait_ge(S["stats6"], n + 1)
                if exists(i, j - 2):
                    n, slot, use, rows = tile(i, j - 2)
                    dve.wait_ge(S["h_ready"], n + 1)
                    add_rows(n, rows, zcols(n)[0:rows], col(noedge, n)[0:rows], steady(i, n, 1))
                if exists(i, j + 3):
                    n, slot, use, rows = tile(i, j + 3)
                    mean_variance(slot, rows)

            def add_rows(n, rows, rows_in, mask, waits):
                if waits:
                    dve.wait_ge(S["acc_ready"], n)
                dve.scalar_tensor_tensor(acc[0:rows, 0, :], rows_in, mask, acc[0:rows, 0, :], ALU.mult,
                                         ALU.add).then_inc(S["acc_ready"], 1)

            dve.wait_ge(S["negb_ready"], 1)
            dve.wait_ge(S["acc_zeroed"], 2)
            node_steps(dve, node_vec, 3, 2)

            dve.wait_ge(rows_loaded[0], 16 * (ET // 4 + 1))
            dve.memset(ring[0:1, 0, :], 0.0).then_inc(S["carry0"], 1)

            def edge_vec(i, j):
                t = 4 * i + j
                if not isinstance(i, int) or j >= 1:
                    dve.wait_ge(S["sum_out"], ET + t)
                    add_rows(NT + t - 1, P, sum_rows[(j - 1) % 4], col(cols[:, 6, :], t - 1), True)
                if not isinstance(i, int) or j < ET:
                    if not isinstance(t, int) or t >= 4:
                        dve.wait_ge(sum1_stored[j % 4], 16 * (i + j // 4))
                        dve.wait_ge(S["sq_ready"], NT + t - 3)
                    for h in range(2):
                        dve.wait_ge(S["sum_done"], 2 * (ET + t) + 1 + h)
                        if not isinstance(t, int) or t < ET - 1:
                            dve.wait_ge(S["carry_ready"], 2 * (ET + t) - 1 + h)
                        last = dve.tensor_tensor(sum_rows[j % 4][:, halves[h]], p_edge(j, h), negb[:, halves[h]], ALU.max)
                    last.then_inc(S["sum_out"], 1)

            edge_steps(dve, edge_vec, 1)

            link(dve.tensor_copy(ident16, ident[:]), "bn_step")
            link(dve.memset(ones3, 1.0), "bn_step")
            dve.wait_ge(S["totals_sum"], 2)
            dve.tensor_copy(bn_rows[1], p_tab[0:1, :]).then_inc(S["square_total_out"], 1)
            dve.wait_ge(S["totals_turned"], 1)
            link(dve.tensor_scalar(WT[:, 0, 0:2 * KD], p_sum[0][:, 0:2 * KD], 1.0 / N, None, ALU.mult), "bn_step")
            link(dve.tensor_tensor(var, mean, mean, ALU.mult), "bn_step")
            dve.tensor_tensor(var, square, var, ALU.subtract).then_inc(S["var_ready"], 1)
            dve.wait_ge(S["bn_root"], 1)
            link(dve.reciprocal(dev, dev), "bn_step")
            link(dve.tensor_tensor(factor, gamma_c, dev, ALU.mult), "bn_step")
            for c in range(KD):
                last = dve.tensor_scalar(diagonal[:, c, :], ident[:], factor[:, c:c + 1], None, ALU.mult)
            last.then_inc(S["diagonal_ready"], 1)
            link(dve.tensor_tensor(shift, mean, factor, ALU.mult), "bn_step")
            link(dve.tensor_tensor(shift, beta_c, shift, ALU.subtract), "bn_step")
            link(dve.tensor_copy(shift_parts[:, :, 0:1], shift.unsqueeze(2)), "bn_step")
            link(dve.tensor_tensor(rest.unsqueeze(2), shift.unsqueeze(2), shift_parts[:, :, 0:1], ALU.subtract), "bn_step")
            link(dve.tensor_copy(shift_parts[:, :, 1:2], rest.unsqueeze(2)), "bn_step")
            dve.tensor_tensor(shift_parts[:, :, 2:3], rest.unsqueeze(2), shift_parts[:, :, 1:2], ALU.subtract
                              ).then_inc(S["parts_ready"], 1)
            dve.wait_ge(S["factor_rows"], 1)

            def out_vec(i, j):
                if exists(i, j + 3):
                    n, slot, use, rows = tile(i, j + 3)
                    if not steady(i, n, X):
                        dve.wait_ge(h_patched[slot], 16)
                    elif not steady(i, n, 2 * X):
                        dve.wait_ge(h_patched_early[slot], 16)
                    else:
                        dve.wait_ge(h_patched[slot], 16 * use)
                    dve.tensor_tensor(zcols(n)[0:rows], zcols(n)[0:rows], p_misc[0:rows, :], ALU.mult).then_inc(S["scaled"], 1)
                if exists(i, j + 1):
                    n, slot, use, rows = tile(i, j + 1)
                    dve.wait_ge(S["res_ready"], n + 1)
                    row_stats(slot, rows, p_out[slot][0:rows, :])
                if exists(i, j):
                    n, slot, use, rows = tile(i, j)
                    reciprocal(n, slot, rows, NT)
                if exists(i, j + 1):
                    dve.wait_ge(S["stats6"], NT + tile(i, j + 1)[0] + 1)
                if exists(i, j):
                    n, slot, use, rows = tile(i, j)
                    shift_of_mean(n, slot, rows, NT)
                if exists(i, j + 1):
                    n, slot, use, rows = tile(i, j + 1)
                    mean_variance(slot, rows)

            node_steps(dve, out_vec, 3, 0, first=2)


_INS = ["x", "src", "dst", "edge_attr_512", "L0_gnn_path_coeffs", "L0_gnn_path_indices", "L1_gnn_W", "L1_gnn_b",
        "L1_gnn_gamma", "L1_gnn_beta"]


def kernel(**inputs):
    import numpy as _np
    import concourse.bacc as _bacc
    from concourse.bass_utils import run_bass_kernel_spmd as _run

    nc = _bacc.Bacc("TRN2", target_bir_lowering=False, num_devices=1)
    arrays, args = {}, []
    for name in _INS:
        a = _np.ascontiguousarray(inputs[name])
        arrays[f"in_{name}"] = a
        args.append(nc.dram_tensor(f"in_{name}", a.shape, mybir.dt.from_np(a.dtype), kind="ExternalInput").ap())
    shape = inputs["x"].shape
    args.append(nc.dram_tensor("out_0", shape, F32, kind="ExternalOutput").ap())
    build(nc, *args)
    r = _run(nc, [arrays], core_ids=[0])
    return r.results[0]["out_0"]
```
